# Optimizing a Trainium2 kernel written in Bass

```python
import numpy as np
import jax
import jax.numpy as jnp

def _softmax(x, axis=-1):
    return jax.nn.softmax(x, axis=axis)

def _gelu(x):
    return jax.nn.gelu(x, approximate=True)

def _silu(x):
    return jax.nn.silu(x)

def _sigmoid(x):
    return jax.nn.sigmoid(x)

def _layernorm(x, axis=-1, eps=1e-05):
    m = jnp.mean(x, axis=axis, keepdims=True)
    v = jnp.var(x, axis=axis, keepdims=True)
    return (x - m) / jnp.sqrt(v + eps)

def _scatter_add(tgt, idx, src, axis=0):
    return tgt.at[idx].add(src)

def _segment_sum(src, seg, n):
    return jax.ops.segment_sum(src, seg, n)
kernel_name = 'mk_sandwich_d1_jaxref_r8_d82a95'

def setup_inputs(seed: int=0):
    np.random.seed(seed)
    _w = jnp.asarray

    def _L0_attn_setup():
        import jax, jax.numpy as jnp
        import numpy as np
        from jax import lax
        CHUNK = 32
        NUM_HEADS = 4
        HEAD_V = 32
        GATE_EPS = 0.02
        RMS_EPS = 1e-05

        def _l2norm(x):
            return x / jnp.sqrt(jnp.sum(x * x, axis=-1, keepdims=True) + 1e-06)

        def _causal_dwconv(x, w):
            k = w.shape[-1]
            lhs = jnp.transpose(x, (0, 2, 1))
            rhs = w[:, None, :]
            y = lax.conv_general_dilated(lhs, rhs, (1,), [(k - 1, 0)], feature_group_count=w.shape[0], dimension_numbers=('NCH', 'OIH', 'NCH'))
            return jnp.transpose(y, (0, 2, 1))

        def _delta_rule_chunkwise(q, k, v, beta):
            b, h, L, dk = q.shape
            dv = v.shape[-1]
            n = L // CHUNK
            q = _l2norm(q)
            k = _l2norm(k)
            v = v * beta[..., None]
            kb = k * beta[..., None]
            ch = lambda t: t.reshape(b, h, n, CHUNK, -1)
            qc, kc, vc, kbc = map(ch, (q, k, v, kb))
            A = jnp.einsum('bhnid,bhnjd->bhnij', kbc, kc)
            eye = jnp.eye(CHUNK, dtype=q.dtype)
            M = eye + jnp.tril(A, -1)
            rhs = jnp.concatenate([vc, kbc], axis=-1)
            sol = lax.linalg.triangular_solve(M, rhs, left_side=True, lower=True, unit_diagonal=True)
            u, w = (sol[..., :dv], sol[..., dv:])

            def step(S, inp):
                q_i, k_i, u_i, w_i = inp
                attn = jnp.tril(jnp.einsum('bhid,bhjd->bhij', q_i, k_i))
                u_adj = u_i - jnp.einsum('bhid,bhde->bhie', w_i, S)
                out_i = jnp.einsum('bhid,bhde->bhie', q_i, S) + attn @ u_adj
                S = S + jnp.einsum('bhid,bhie->bhde', k_i, u_adj)
                return (S, out_i)
            mv = lambda t: jnp.moveaxis(t, 2, 0)
            S0 = jnp.zeros((b, h, dk, dv), q.dtype)
            S, outs = lax.scan(step, S0, (mv(qc), mv(kc), mv(u), mv(w)))
            out = jnp.moveaxis(outs, 0, 2).reshape(b, h, L, dv)
            return (out, S)

        def _forward(hidden_states, w_q, w_k, w_v, w_b, conv_q_w, conv_k_w, conv_v_w, fir1, fir3, fir7, fir15, fir31, gate_w1, gate_b1, gate_w2, gate_b2, norm_w, w_o):
            b, l, _ = hidden_states.shape
            H, Dv = (NUM_HEADS, HEAD_V)
            silu = jax.nn.silu
            q = silu(_causal_dwconv(hidden_states @ w_q, conv_q_w))
            k = silu(_causal_dwconv(hidden_states @ w_k, conv_k_w))
            v = silu(_causal_dwconv(hidden_states @ w_v, conv_v_w))
            beta = jax.nn.sigmoid(hidden_states @ w_b)
            to_bhl = lambda t: jnp.transpose(t.reshape(b, l, H, -1), (0, 2, 1, 3))
            delta_out, _S = _delta_rule_chunkwise(to_bhl(q), to_bhl(k), to_bhl(v), jnp.transpose(beta, (0, 2, 1)))
            delta_out = jnp.transpose(delta_out, (0, 2, 1, 3))
            v4 = v.reshape(b, l, H, Dv)
            firs = [_causal_dwconv(v, f).reshape(b, l, H, Dv) for f in (fir1, fir3, fir7, fir15, fir31)]
            streams = firs + [delta_out, v4]
            stats = jnp.concatenate([jnp.mean(jnp.abs(s), axis=-1) for s in streams], axis=-1)
            gate_inp = jnp.concatenate([hidden_states, stats], axis=-1)
            hmid = jax.nn.gelu(gate_inp @ gate_w1 + gate_b1, approximate=False)
            logits = (hmid @ gate_w2 + gate_b2).reshape(b, l, H, len(streams))
            wts = jax.nn.softplus(logits) + GATE_EPS
            wts = wts / jnp.sum(wts, axis=-1, keepdims=True)
            stacked = jnp.stack(streams, axis=-2)
            o = jnp.einsum('blhsd,blhs->blhd', stacked, wts)
            o = o * lax.rsqrt(jnp.mean(o * o, axis=-1, keepdims=True) + RMS_EPS) * norm_w
            return o.reshape(b, l, H * Dv) @ w_o
        key = jax.random.key(seed)
        ks = jax.random.split(key, 20)
        D = 128
        n = lambda i, shape, s=0.02: jax.random.normal(ks[i], shape, jnp.float32) * s
        return {'hidden_states': jax.random.normal(ks[0], (4, 512, D), jnp.float32), 'w_q': n(1, (D, D)), 'w_k': n(2, (D, D)), 'w_v': n(3, (D, D)), 'w_b': n(4, (D, NUM_HEADS)), 'conv_q_w': n(5, (D, 4), 0.2), 'conv_k_w': n(6, (D, 4), 0.2), 'conv_v_w': n(7, (D, 4), 0.2), 'fir1': n(8, (D, 1), 0.2), 'fir3': n(9, (D, 3), 0.2), 'fir7': n(10, (D, 7), 0.2), 'fir15': n(11, (D, 15), 0.2), 'fir31': n(12, (D, 31), 0.2), 'gate_w1': n(13, (D + NUM_HEADS * 7, 2 * D)), 'gate_b1': n(14, (2 * D,)), 'gate_w2': n(15, (2 * D, NUM_HEADS * 7)), 'gate_b2': n(16, (NUM_HEADS * 7,)) + 0.5, 'norm_w': 1.0 + n(17, (HEAD_V,)), 'w_o': n(18, (D, D))}
    _L0_attn_in = _L0_attn_setup()

    def _L0_ffn_setup():
        import jax, jax.numpy as jnp
        import numpy as np
        B, S, D = (2, 128, 128)
        H = 64
        E = 16
        K = 2
        HS = 2 * H
        ROUTE_SCALE = 1.0

        def _gated_mlp_act(y):
            u, g = jnp.split(y, 2, axis=-1)
            return u * jax.nn.silu(g)
        key = jax.random.key(seed)
        ks = jax.random.split(key, 6)
        s = 0.02
        return {'x': jax.random.normal(ks[0], (B, S, D), dtype=jnp.float32), 'Wg': jax.random.normal(ks[1], (E, D), dtype=jnp.float32) * s, 'W1': jax.random.normal(ks[2], (E, D, 2 * H), dtype=jnp.float32) * s, 'W2': jax.random.normal(ks[3], (E, H, D), dtype=jnp.float32) * s, 'Ws1': jax.random.normal(ks[4], (D, 2 * HS), dtype=jnp.float32) * s, 'Ws2': jax.random.normal(ks[5], (HS, D), dtype=jnp.float32) * s}
    _L0_ffn_in = _L0_ffn_setup()
    _d = {'L0_attn_hidden_states': _L0_attn_in['hidden_states'], 'L0_attn_w_q': _L0_attn_in['w_q'], 'L0_attn_w_k': _L0_attn_in['w_k'], 'L0_attn_w_v': _L0_attn_in['w_v'], 'L0_attn_w_b': _L0_attn_in['w_b'], 'L0_attn_conv_q_w': _L0_attn_in['conv_q_w'], 'L0_attn_conv_k_w': _L0_attn_in['conv_k_w'], 'L0_attn_conv_v_w': _L0_attn_in['conv_v_w'], 'L0_attn_fir1': _L0_attn_in['fir1'], 'L0_attn_fir3': _L0_attn_in['fir3'], 'L0_attn_fir7': _L0_attn_in['fir7'], 'L0_attn_fir15': _L0_attn_in['fir15'], 'L0_attn_fir31': _L0_attn_in['fir31'], 'L0_attn_gate_w1': _L0_attn_in['gate_w1'], 'L0_attn_gate_b1': _L0_attn_in['gate_b1'], 'L0_attn_gate_w2': _L0_attn_in['gate_w2'], 'L0_attn_gate_b2': _L0_attn_in['gate_b2'], 'L0_attn_norm_w': _L0_attn_in['norm_w'], 'L0_attn_w_o': _L0_attn_in['w_o'], 'L0_ffn_Wg': _L0_ffn_in['Wg'], 'L0_ffn_W1': _L0_ffn_in['W1'], 'L0_ffn_W2': _L0_ffn_in['W2'], 'L0_ffn_Ws1': _L0_ffn_in['Ws1'], 'L0_ffn_Ws2': _L0_ffn_in['Ws2']}
    _x0 = _d['L0_attn_hidden_states']
    _d['L0_attn_hidden_states'] = jax.random.normal(jax.random.fold_in(jax.random.key(seed), 1), (2, 1024, 128), dtype=_x0.dtype)
    del _x0
    return _d

def reference(L0_attn_hidden_states, L0_attn_w_q, L0_attn_w_k, L0_attn_w_v, L0_attn_w_b, L0_attn_conv_q_w, L0_attn_conv_k_w, L0_attn_conv_v_w, L0_attn_fir1, L0_attn_fir3, L0_attn_fir7, L0_attn_fir15, L0_attn_fir31, L0_attn_gate_w1, L0_attn_gate_b1, L0_attn_gate_w2, L0_attn_gate_b2, L0_attn_norm_w, L0_attn_w_o, L0_ffn_Wg, L0_ffn_W1, L0_ffn_W2, L0_ffn_Ws1, L0_ffn_Ws2):

    def _L0_attn_ref(hidden_states, w_q, w_k, w_v, w_b, conv_q_w, conv_k_w, conv_v_w, fir1, fir3, fir7, fir15, fir31, gate_w1, gate_b1, gate_w2, gate_b2, norm_w, w_o):
        import jax, jax.numpy as jnp
        import numpy as np
        from jax import lax
        CHUNK = 32
        NUM_HEADS = 4
        HEAD_V = 32
        GATE_EPS = 0.02
        RMS_EPS = 1e-05

        def _l2norm(x):
            return x / jnp.sqrt(jnp.sum(x * x, axis=-1, keepdims=True) + 1e-06)

        def _causal_dwconv(x, w):
            k = w.shape[-1]
            lhs = jnp.transpose(x, (0, 2, 1))
            rhs = w[:, None, :]
            y = lax.conv_general_dilated(lhs, rhs, (1,), [(k - 1, 0)], feature_group_count=w.shape[0], dimension_numbers=('NCH', 'OIH', 'NCH'))
            return jnp.transpose(y, (0, 2, 1))

        def _delta_rule_chunkwise(q, k, v, beta):
            b, h, L, dk = q.shape
            dv = v.shape[-1]
            n = L // CHUNK
            q = _l2norm(q)
            k = _l2norm(k)
            v = v * beta[..., None]
            kb = k * beta[..., None]
            ch = lambda t: t.reshape(b, h, n, CHUNK, -1)
            qc, kc, vc, kbc = map(ch, (q, k, v, kb))
            A = jnp.einsum('bhnid,bhnjd->bhnij', kbc, kc)
            eye = jnp.eye(CHUNK, dtype=q.dtype)
            M = eye + jnp.tril(A, -1)
            rhs = jnp.concatenate([vc, kbc], axis=-1)
            sol = lax.linalg.triangular_solve(M, rhs, left_side=True, lower=True, unit_diagonal=True)
            u, w = (sol[..., :dv], sol[..., dv:])

            def step(S, inp):
                q_i, k_i, u_i, w_i = inp
                attn = jnp.tril(jnp.einsum('bhid,bhjd->bhij', q_i, k_i))
                u_adj = u_i - jnp.einsum('bhid,bhde->bhie', w_i, S)
                out_i = jnp.einsum('bhid,bhde->bhie', q_i, S) + attn @ u_adj
                S = S + jnp.einsum('bhid,bhie->bhde', k_i, u_adj)
                return (S, out_i)
            mv = lambda t: jnp.moveaxis(t, 2, 0)
            S0 = jnp.zeros((b, h, dk, dv), q.dtype)
            S, outs = lax.scan(step, S0, (mv(qc), mv(kc), mv(u), mv(w)))
            out = jnp.moveaxis(outs, 0, 2).reshape(b, h, L, dv)
            return (out, S)

        def _forward(hidden_states, w_q, w_k, w_v, w_b, conv_q_w, conv_k_w, conv_v_w, fir1, fir3, fir7, fir15, fir31, gate_w1, gate_b1, gate_w2, gate_b2, norm_w, w_o):
            b, l, _ = hidden_states.shape
            H, Dv = (NUM_HEADS, HEAD_V)
            silu = jax.nn.silu
            q = silu(_causal_dwconv(hidden_states @ w_q, conv_q_w))
            k = silu(_causal_dwconv(hidden_states @ w_k, conv_k_w))
            v = silu(_causal_dwconv(hidden_states @ w_v, conv_v_w))
            beta = jax.nn.sigmoid(hidden_states @ w_b)
            to_bhl = lambda t: jnp.transpose(t.reshape(b, l, H, -1), (0, 2, 1, 3))
            delta_out, _S = _delta_rule_chunkwise(to_bhl(q), to_bhl(k), to_bhl(v), jnp.transpose(beta, (0, 2, 1)))
            delta_out = jnp.transpose(delta_out, (0, 2, 1, 3))
            v4 = v.reshape(b, l, H, Dv)
            firs = [_causal_dwconv(v, f).reshape(b, l, H, Dv) for f in (fir1, fir3, fir7, fir15, fir31)]
            streams = firs + [delta_out, v4]
            stats = jnp.concatenate([jnp.mean(jnp.abs(s), axis=-1) for s in streams], axis=-1)
            gate_inp = jnp.concatenate([hidden_states, stats], axis=-1)
            hmid = jax.nn.gelu(gate_inp @ gate_w1 + gate_b1, approximate=False)
            logits = (hmid @ gate_w2 + gate_b2).reshape(b, l, H, len(streams))
            wts = jax.nn.softplus(logits) + GATE_EPS
            wts = wts / jnp.sum(wts, axis=-1, keepdims=True)
            stacked = jnp.stack(streams, axis=-2)
            o = jnp.einsum('blhsd,blhs->blhd', stacked, wts)
            o = o * lax.rsqrt(jnp.mean(o * o, axis=-1, keepdims=True) + RMS_EPS) * norm_w
            return o.reshape(b, l, H * Dv) @ w_o
        return _forward(hidden_states, w_q, w_k, w_v, w_b, conv_q_w, conv_k_w, conv_v_w, fir1, fir3, fir7, fir15, fir31, gate_w1, gate_b1, gate_w2, gate_b2, norm_w, w_o)

    def _L0_ffn_ref(x, Wg, W1, W2, Ws1, Ws2):
        import jax, jax.numpy as jnp
        import numpy as np
        B, S, D = (2, 128, 128)
        H = 64
        E = 16
        K = 2
        HS = 2 * H
        ROUTE_SCALE = 1.0

        def _gated_mlp_act(y):
            u, g = jnp.split(y, 2, axis=-1)
            return u * jax.nn.silu(g)
        x_shape = x.shape
        xf = x.reshape(-1, D)
        scores = jax.nn.softmax(xf @ Wg.T, axis=-1)
        wk, idx = jax.lax.top_k(scores, K)
        wk = wk * ROUTE_SCALE
        cw = jnp.sum(jax.nn.one_hot(idx, E, dtype=xf.dtype) * wk[..., None], axis=1)
        h = _gated_mlp_act(jnp.einsum('td,edh->teh', xf, W1))
        z = jnp.einsum('te,teh,ehd->td', cw, h, W2)
        ys = _gated_mlp_act(xf @ Ws1) @ Ws2
        return (z + ys).reshape(x_shape)
    x = L0_attn_hidden_states
    x = x + _layernorm(_L0_attn_ref(_layernorm(x, axis=-1), L0_attn_w_q, L0_attn_w_k, L0_attn_w_v, L0_attn_w_b, L0_attn_conv_q_w, L0_attn_conv_k_w, L0_attn_conv_v_w, L0_attn_fir1, L0_attn_fir3, L0_attn_fir7, L0_attn_fir15, L0_attn_fir31, L0_attn_gate_w1, L0_attn_gate_b1, L0_attn_gate_w2, L0_attn_gate_b2, L0_attn_norm_w, L0_attn_w_o), axis=-1)
    x = x + _layernorm(_L0_ffn_ref(_layernorm(x, axis=-1), L0_ffn_Wg, L0_ffn_W1, L0_ffn_W2, L0_ffn_Ws1, L0_ffn_Ws2), axis=-1)
    return x

_drawn_inputs = setup_inputs


def setup_inputs(seed=0):
    import zlib

    import numpy as np

    out = dict(_drawn_inputs(seed))
    spreads = {}
    factors = {'L0_attn_gate_w1': 3.108,
     'L0_attn_gate_b1': 22.702,
     'L0_attn_gate_w2': 3.129,
     'L0_attn_gate_b2': 6.661,
     'L0_attn_norm_w': 20.469}
    for name, (base, spread) in spreads.items():
        noise = np.random.default_rng([zlib.crc32(name.encode()), seed]).standard_normal(out[name].shape)
        drawn = base * np.exp(spread * noise) if base else spread * noise
        out[name] = jnp.asarray(drawn.astype(out[name].dtype))
    for name, factor in factors.items():
        out[name] = (out[name] * factor).astype(out[name].dtype)
    return out
```

```python
import concourse.bass as bass
from concourse import mybir
from contextlib import ExitStack
import numpy as np

NB, SEQ, D = 2, 1024, 128
H, DH, C = 4, 32, 32
TILES = 4
TB = SEQ // TILES
TT = NB * TB
NCH = TB // C
G = NB * NCH
A = 4
Q = TB // A
FIRS = (31, 15, 7, 3)
MS = [(k + 3 + 3) // 4 for k in FIRS]
MX = MS[0]
NS = 7
STREAM = (4, 3, 2, 1, 0, 5, 6)
E, HE, HS = 16, 64, 128
PAIRS = E // 2
LN_EPS, L2_EPS, RMS_EPS, GATE_EPS = 1e-5, 1e-6, 1e-5, 0.02
LEVELS = 5

C_ID = 0
C_ONES = 128
C_I32 = 256
C_LOW = 288
C_UP = 320
C_LEV = 352
C_HEAD = 512
C_SEL = 512 + 1024
C_END = C_SEL + PAIRS * 128


def shape_constants():
    c = np.zeros((128, C_END), np.float32)
    p, j, r = np.arange(128)[:, None], np.arange(32)[None, :], np.arange(128)[None, :]
    i = p % 32
    c[:, C_ID:C_ID + 128] = p == r
    c[:, C_ONES:C_ONES + 128] = p // 32 == r // 32
    c[:, C_I32:C_I32 + 32] = i == j
    c[:, C_LOW:C_LOW + 32] = j < i
    c[:, C_UP:C_UP + 32] = i <= j
    for l in range(LEVELS):
        s = 1 << l
        c[:, C_LEV + 32 * l:C_LEV + 32 * l + 32] = (i // (2 * s) == j // (2 * s)) & (i // s % 2 == 1) & (j // s % 2 == 0)
    for t in range(2 * A):
        c[:32, C_HEAD + 128 * t:C_HEAD + 128 * t + 128] = p[:32] == H * t + r // DH
    for t in range(PAIRS):
        c[:48, C_SEL + 128 * t:C_SEL + 128 * t + 128] = (p[:48] % 16) == 2 * t + r // 64
    return c


def build(nc, x_in, w_q, w_k, w_v, w_b, conv_q, conv_k, conv_v, fir1, fir3, fir7, fir15, fir31,
          gate_w1, gate_b1, gate_w2, gate_b2, norm_w, w_o, Wg, W1, W2, Ws1, Ws2, consts, out):
    f32, bf16 = mybir.dt.float32, mybir.dt.bfloat16
    ALU, ACT, AX = mybir.AluOpType, mybir.ActivationFunctionType, mybir.AxisListType

    ctx = ExitStack()
    with ctx:
        def sb(name, shape, dt=f32):
            return ctx.enter_context(nc.sbuf_tensor(name, shape, dt))

        def sem(name):
            return ctx.enter_context(nc.semaphore(name))

        cst = sb("cst", [128, C_HEAD])
        ident = cst[:, C_ID:C_ID + 128]
        ones_head = cst[:, C_ONES:C_ONES + 128]
        eye32 = cst[:, C_I32:C_I32 + 32]
        low = cst[:, C_LOW:C_LOW + 32]
        up = cst[:, C_UP:C_UP + 32]
        headsel = sb("headsel", [32, 2 * A, 128])
        selb = sb("selb", [48, PAIRS, 128], bf16)
        identb = sb("identb", [128, 128], bf16)
        ffn = sb("ffn", [128, 6, TT])
        sg, sc, hT = ffn[:, 0:2, :], ffn[:, 2:4, :], ffn[:, 4:6, :]
        diag = ffn[:, 0:3, :].rearrange("p i (t n) -> p i t n", t=4)
        wraw = ffn[:, 3, 0:384].rearrange("p (i n) -> p i n", i=3)
        wrawT = ffn[:, 4, 0:384].rearrange("p (i n) -> p i n", i=3)
        convw = sb("convw", [128, 3, 4])
        wtap = sb("wtap", [128, 3, 4, 128])
        wb_raw = sb("wb_raw", [128, H])
        wb_rep = sb("wb_rep", [128, H, 32])
        firw = [sb(f"firw{s}", [128, H, 4 * MS[s]]) for s in range(4)]
        toep = [sb(f"toep{m}", [128, H, sum(m < x for x in MS), A, 32]) for m in range(MX)]
        fir1_row = sb("fir1_row", [128, 128])
        g1x = sb("g1x", [128, 2 * D])
        g1s = sb("g1s", [NS * H, 2 * D])
        gb1 = sb("gb1", [128, 2])
        g2raw = sb("g2raw", [128, 2, NS * H])
        g2 = sb("g2", [128, 2, NS, H])
        gb2raw = sb("gb2raw", [128, NS * H])
        gb2 = sb("gb2", [128, NS, H])
        normw = sb("normw", [128, 1])
        wo_raw = ffn[:, 5, 0:128]
        wo = sb("wo", [128, 128])
        wg_raw = sb("wg_raw", [E, 128])
        wgT = sb("wgT", [128, E])
        w1 = sb("w1", [128, PAIRS, 2, 2, HE])
        w2 = sb("w2", [128, PAIRS, 128])
        ws1 = sb("ws1", [128, 2 * HS])
        ws2 = sb("ws2", [128, 128])
        one = sb("one", [128, 1])

        x_all = sb("x_all", [128, TILES, A, 128])
        st = sb("st", [128, A, 6])
        mv = sb("mv", [128, A, 2])
        rs = sb("rs", [128, 3, 2 * A * H])
        rnT = sb("rnT", [2 * A * H, 128])
        spare = sb("spare", [1, 1])
        xn = sb("xn", [128, A, 128])
        xnT = sb("xnT", [128, NB, 3 + TB])
        kqs = sb("kqs", [128, 2, TT])
        vF = sb("vF", [128, TT])
        vP = sb("vP", [128, TT])
        sq = sb("sq", [128, 2, TT])
        kq = sb("kq", [128, G, 2, C])
        beta = sb("beta", [128, TT])
        betaB = sb("betaB", [128, G, C])
        v4 = sb("v4", [128, H, 8 + Q, NB])
        vB = sb("vB", [128, G, C])
        Lc = sb("Lc", [128, G, C])
        LT = sb("LT", [128, G, C])
        X = sb("X", [128, G, C])
        XT = sb("XT", [128, G, C])
        M1 = sb("M1", [128, G, C])
        kB = M1
        tmpB = M1
        attnT = sb("attnT", [128, G, C])
        KTbd = sb("KTbd", [128, G, 128])
        Kbd = sb("Kbd", [128, G, 128])
        QTbd = sb("QTbd", [128, G, 128])
        LTbd = sb("LTbd", [128, G, 128])
        XTbd = sb("XTbd", [128, G, 128])
        ATbd = LTbd
        S = sb("S", [128, 2, NB, DH])
        r = sb("r", [128, NB, DH])
        u = sb("u", [128, NB, DH])
        oB = Lc
        oF = vP
        SM = sb("SM", [128, NS, A, H, DH])
        stat = sb("stat", [128, A, NS, H])
        statT = ffn[0:NS * H, 2, :]
        hid = ffn[:, 0:2, :]
        z = sb("z", [128, A, NS * H])
        za = sb("za", [128, A, NS * H])
        ze = sb("ze", [128, A, NS * H])
        zl = sb("zl", [128, A, NS * H])
        wt = sb("wt", [128, A, NS, H])
        wsum = sb("wsum", [128, A, H])
        prod = hid.rearrange("p i (a h c) -> p i a h c", a=A, h=H)
        acc = kqs[:, :, :].rearrange("p i (a h c) -> p i a h c", a=A, h=H)
        ss = sb("ss", [128, A, H])
        oT = sb("oT", [128, TT])
        y1 = sb("y1", [128, A, 128])
        x1 = sb("x1", [128, A, 128])
        x2n = y1
        x2T = sb("x2T", [128, TT])
        rl = sb("rl", [128, A, E])
        top8 = sb("top8", [128, A, 8])
        want2 = sb("want2", [128, A, 8])
        rrep = sb("rrep", [128, A, E])
        re = sb("re", [128, A, E])
        rsum = sb("rsum", [128, A])
        cw = sb("cw", [128, A, E])
        cwr = sb("cwr", [128, 2, A, E])
        cw3 = sb("cw3", [128, A, 8, E], bf16)
        cwT = sb("cwT", [48, TT], bf16)
        zT = oT

        PS = ctx.enter_context(nc.psum_tensor("PS", [128, 8 * 512], f32))

        def bank(i, n=1):
            return PS[:, 512 * i:512 * (i + n)]

        w_in = sem("w_in")
        x_in_done = sem("x_in_done")
        init = sem("init")
        wprep_pe = sem("wprep_pe")
        wprep = sem("wprep")
        toep_ready = sem("toep_ready")
        dve = sem("dve")
        poolc = sem("poolc")
        names = """xn_ready xnT_ps xnT_ready qkv_ps beta_ps silu_done beta_exp sq_done ssq_ps kq_ready
            bd_ready gram_ps L_ready m1_ps m1_ready m2_ps xt_ready scan_ready
            ks_ps r_ready u_ps u_ready ds_ps s_ready o_ps oF_ready fir_ps fir_out
            tm_ps tm_out stat_ready statT_ps statT_ready hid_ps hid_ready logit_ps z_ready zabs rn_ready rnT_ps rnT_ready rnF_ps z_exp z_ln
            v4_ready o_ready oT_ps oT_ready y_ps x2_ready x2T_ps x2T_ready router_ps re_in re_out
            cw_ready cwT_ps cwT_ready up_ps sg_ready h_ready z_ps zT_ready yo_ps y_ready y_stored
            wts_ready mix_in sqo""".split()
        s = {n: sem(n) for n in names}

        block = ctx.enter_context(nc.Block())

        x_v = x_in.rearrange("b (t q a) d -> b q t (a d)", t=TILES, a=A)
        o_v = out.rearrange("b (t q a) d -> b q t (a d)", t=TILES, a=A)

        loads = [
            (cst[:, :], consts[:, 0:C_HEAD]), (headsel[:, :, :], consts[0:32, C_HEAD:C_SEL].rearrange("p (t n) -> p t n", n=128)), (kqs[:, :, :], consts[:, C_SEL:C_END].rearrange("p (i n) -> p i n", i=2)), (wraw[:, 0, :], w_q), (wraw[:, 1, :], w_k), (wraw[:, 2, :], w_v),
            (convw[:, 0, :], conv_q), (convw[:, 1, :], conv_k), (convw[:, 2, :], conv_v),
            (wb_raw[:, :], w_b), (fir1_row[:, :], fir1.rearrange("c k -> (c k)").partition_broadcast(128)),
            (g1x[:, :], gate_w1[0:D, :]),
            (gb1[:, :], gate_b1.rearrange("(a p) -> p a", p=128)),
            (g2raw[:, :, :], gate_w2.rearrange("(a p) n -> p a n", p=128)),
            (gb2raw[:, :], gate_b2.partition_broadcast(128)),
            (wo_raw[:, :], w_o), (wg_raw[:, :], Wg),
            (w2[:, :, :], W2.rearrange("(t e) h d -> (e h) t d", e=2)),
            (ws1[:, :], Ws1), (ws2[:, :], Ws2),
        ]
        loads += [(g1s[4 * i:4 * i + 4, :], gate_w1[D + 4 * STREAM[i]:D + 4 * STREAM[i] + 4, :]) for i in range(NS)]
        loads += [(normw[32 * h:32 * h + 32, :], norm_w.rearrange("(c a) -> c a", a=1)) for h in range(H)]
        loads += [(w1[:, :, i, e, :], W1.rearrange("(t e) d (i h) -> i e d t h", e=2, i=2)[i, e]) for i in range(2) for e in range(2)]
        WTOTAL = 16 * len(loads)

        @block.gpsimd
        def _(eng):
            for b in (KTbd, Kbd, QTbd, LTbd, XTbd):
                eng.memset(b[:, :, :], 0.0).then_inc(init, 1)
            eng.memset(S[:, :, :, :], 0.0).then_inc(s["s_ready"], 1)
            eng.memset(xnT[:, :, :], 0.0).then_inc(init, 1)
            eng.memset(v4[:, :, :, :], 0.0).then_inc(init, 1)
            eng.memset(one[:, :], 1.0).then_inc(init, 1)
            eng.memset(cw3[:, :, :, :], 0.0).then_inc(init, 1)
            for i in range(4):
                eng.memset(firw[i][:, :, :], 0.0).then_inc(init, 1)
            eng.wait_ge(init, 13)
            with nc.allow_non_contiguous_dma("short rows of taps"):
                for i, w in enumerate((fir31, fir15, fir7, fir3)):
                    for b in range(4):
                        eng.dma_start(firw[i][32 * b:32 * b + 32, :, 5 - b:5 - b + FIRS[i]],
                                      w.rearrange("(h c) k -> c h k", h=H)).then_inc(poolc, 16)
            eng.wait_ge(poolc, 256)
            eng.wait_ge(w_in, WTOTAL)
            for m in range(MX):
                for i in range(4):
                    if m < MS[i]:
                        for a in range(A):
                            zp = 4 * MS[i] - 1 - 4 * m - a
                            t = eng.tensor_tensor(
                                out=toep[m][:, :, i, a, :],
                                in0=eye32.unsqueeze(1).to_broadcast([128, H, 32]),
                                in1=firw[i][:, :, zp:zp + 1].to_broadcast([128, H, 32]),
                                op=ALU.mult)
            t.then_inc(toep_ready, 1)
            with eng.Fori(0, TILES) as k:
                eng.wait_ge(s["tm_out"], 2 * k + 1)
                eng.tensor_tensor(out=SM[:, 4, :, :, :], in0=SM[:, 6, :, :, :],
                                  in1=fir1_row[:, :].rearrange("p (h c) -> p h c", h=H).unsqueeze(1)
                                  .to_broadcast([128, A, H, DH]), op=ALU.mult).then_inc(s["mix_in"], 1)

        @block.sync
        def _(eng):
            with nc.allow_non_contiguous_dma("weights, once"):
                for dst, src in loads:
                    eng.dma_start(dst, src).then_inc(w_in, 16)
            with eng.Fori(0, TILES) as k:
                eng.wait_ge(s["y_ready"], k + 1)
                for b in range(NB):
                    eng.dma_start(o_v[b, :, bass.ds(k, 1), :], x_all[b:128:2, bass.ds(k, 1), :, :].rearrange("p k a d -> p (k a) d")).then_inc(s["y_stored"], 16)
            eng.wait_ge(s["y_stored"], 32 * TILES)

        @block.scalar
        def _(eng):
            for t in range(TILES):
                for b in range(NB):
                    eng.dma_start(x_all[b:128:2, t, :, :],
                                  x_v[b, :, t, :]).then_inc(x_in_done, 16)
            eng.wait_ge(w_in, WTOTAL)
            eng.wait_ge(init, 13)
            with eng.Fori(0, TILES) as k:
                eng.wait_ge(s["qkv_ps"], k + 1)
                eng.activation(kqs[:, 0, :], bank(1), ACT.Silu)
                eng.activation(kqs[:, 1, :], bank(2), ACT.Silu)
                eng.activation(vP[:, :].rearrange("p (a q b) -> p b q a", a=A, b=NB),
                               bank(3).rearrange("p (b q a) -> p b q a", a=A, b=NB), ACT.Silu)
                eng.activation(vF[:, :], bank(3), ACT.Silu).then_inc(s["silu_done"], 1)
                eng.wait_ge(s["silu_done"], k + 1)
                eng.activation(sq[:, :, :], kqs[:, :, :], ACT.Square).then_inc(s["sq_done"], 1)
                eng.wait_ge(s["beta_ps"], k + 1)
                eng.activation(beta[:, :], bank(4), ACT.Tanh, scale=0.5).then_inc(s["beta_exp"], 1)
                for h in range(H):
                    eng.wait_ge(s["fir_ps"], 4 * k + h + 1)
                    eng.activation(SM[:, 0:4, :, h, :],
                                   bank(1 + h % 2).rearrange("p (s a c) -> p s a c", s=4, a=A),
                                   ACT.Copy).then_inc(s["fir_out"], 1)
                for i, strm in enumerate((6, 5)):
                    eng.wait_ge(s["tm_ps"], 2 * k + i + 1)
                    eng.activation(SM[:, strm, :, :, :].rearrange("p a h c -> p (a h c)"), bank(0),
                                   ACT.Copy).then_inc(s["tm_out"], 1)
                eng.wait_ge(s["statT_ps"], k + 1)
                eng.activation(statT.rearrange("s (b q a) -> s a q b", b=NB, a=A),
                               bank(0)[0:NS * H, :].rearrange("s (a q b) -> s a q b", a=A, b=NB),
                               ACT.Copy, scale=1.0 / DH).then_inc(s["statT_ready"], 1)
                for i in range(2):
                    eng.wait_ge(s["hid_ps"], 2 * k + i + 1)
                    eng.activation(hid[:, i, :].rearrange("p (a q b) -> p b q a", a=A, b=NB),
                                   bank(1 + i).rearrange("p (b q a) -> p b q a", a=A, b=NB), ACT.Gelu, bias=gb1[:, i:i + 1]).then_inc(s["hid_ready"], 1)
                eng.wait_ge(s["z_ready"], k + 1)
                eng.activation(za[:, :, :], z[:, :, :], ACT.Abs).then_inc(s["zabs"], 1)
                eng.wait_ge(s["zabs"], k + 1)
                eng.activation(ze[:, :, :], za[:, :, :], ACT.Exp, scale=-1.0).then_inc(s["z_exp"], 1)
                eng.wait_ge(s["z_exp"], k + 1)
                eng.activation(zl[:, :, :], ze[:, :, :], ACT.Ln, bias=one[:, :]).then_inc(s["z_ln"], 1)
                eng.wait_ge(s["re_in"], k + 1)
                eng.activation(re[:, :, :], rrep[:, :, :], ACT.Exp).then_inc(s["re_out"], 1)
                for j in range(PAIRS + 1):
                    n = (PAIRS + 1) * k + j
                    eng.wait_ge(s["up_ps"], n + 1)
                    if j >= 2:
                        eng.wait_ge(s["h_ready"], n - 1)
                    eng.activation(sg[:, j % 2, :], bank(2 + 3 * (j % 2)), ACT.Silu).then_inc(s["sg_ready"], 1)

        @block.vector
        def _(eng):
            CH = DVE_STEPS
            cnt = [0]
            base = [0]
            kk = [0]

            def carry_wait():
                V.memset(spare[0:1, 0:1], 0.0)

            def link(ins):
                cnt[0] += 1
                ins.then_inc(dve, 1)
                eng.wait_ge(dve, base[0] + cnt[0])

            V = nc.vector

            def expand(dst, src, sem_=None):
                for h in range(H):
                    t = V.tensor_copy(dst[32 * h:32 * h + 32, :, 32 * h:32 * h + 32],
                                      src[32 * h:32 * h + 32, :, :])
                return t

            def bc(ap, n=G):
                return ap.unsqueeze(1).to_broadcast([128, n, 32])

            def inv_sqrt(n):
                v, y, t = rs[:, 0, 0:n], rs[:, 1, 0:n], rs[:, 2, 0:n]
                i32 = mybir.dt.int32
                link(V.tensor_scalar(y.bitcast(i32), v.bitcast(i32), 1, None, ALU.logical_shift_right))
                link(V.tensor_scalar(y.bitcast(i32), y.bitcast(i32), -1.0, float(0x5F3759DF), ALU.mult, ALU.add))
                for _ in range(4):
                    link(V.tensor_tensor(t, y, y, ALU.mult))
                    link(V.scalar_tensor_tensor(out=t, in0=t, scalar=-0.5, in1=v, op0=ALU.mult, op1=ALU.mult))
                    link(V.scalar_tensor_tensor(out=y, in0=t, scalar=1.5, in1=y, op0=ALU.add, op1=ALU.mult))

            def layer_norm(src, dst, eps_=LN_EPS):
                for a in range(A):
                    t = V.bn_stats(st[:, a, :], src(a))
                link(t)
                carry_wait()
                for a in range(A):
                    t = V.bn_aggr(mv[:, a, :], st[:, a, :])
                link(t)
                link(V.tensor_scalar(rs[:, 0, 0:A], mv[:, :, 1], eps_, None, ALU.add))
                inv_sqrt(A)
                for a in range(A):
                    t = V.tensor_scalar(dst[:, a, :], src(a), mv[:, a, 0:1], rs[:, 1, a:a + 1],
                                        ALU.subtract, ALU.mult)
                return t

            eng.wait_ge(w_in, WTOTAL)
            eng.wait_ge(init, 13)
            V.tensor_copy(identb[:, :], ident)
            V.tensor_copy(selb[:, :, :], kqs[0:48, :, :].rearrange("e i n -> e (i n)").rearrange("e (t p) -> e t p", t=PAIRS))
            V.tensor_copy(wb_rep[:, :, :], wb_raw[:, :].unsqueeze(2).to_broadcast([128, H, 32]))
            V.tensor_scalar(wo[:, :], wo_raw[:, :], normw[:, 0:1], None, ALU.mult)
            for i in range(NS):
                V.tensor_copy(g2[:, :, i, :], g2raw[:, :, STREAM[i]::NS])
                V.tensor_copy(gb2[:, i, :], gb2raw[:, STREAM[i]::NS])
            for i in range(3):
                for t in range(4):
                    last = V.tensor_scalar(diag[:, i, t, :], ident, convw[:, i, t:t + 1], None, ALU.mult)
            last.then_inc(wprep, 1)
            eng.wait_ge(wprep_pe, 1)
            V.tensor_copy(wrawT[:, :, :], bank(0)[:, 0:384].rearrange("p (i n) -> p i n", i=3))
            V.tensor_copy(wgT[:, :], bank(0)[:, 384:400]).then_inc(wprep, 1)
            for i in range(3):
                eng.wait_ge(wprep_pe, 2 + i)
                V.tensor_copy(wtap[:, i, :, :], bank(1 + i).rearrange("p (t n) -> p t n", t=4)).then_inc(wprep, 1)

            with eng.Fori(0, TILES) as k:
                base[0] = CH * k
                kk[0] = k
                cnt[0] = 0
                eng.wait_ge(x_in_done, 32 * TILES)
                layer_norm(lambda a: x_all[:, bass.ds(k, 1), a, :].rearrange("p k d -> p (k d)"), xn).then_inc(s["xn_ready"], 1)
                link(V.tensor_copy(xnT[:, :, 0:3], xnT[:, :, TB:TB + 3]))
                eng.wait_ge(s["xnT_ps"], k + 1)
                V.tensor_copy(xnT[:, :, 3:3 + TB].rearrange("p b (q a) -> p a q b", a=A),
                              bank(0).rearrange("p (a q b) -> p a q b", a=A, b=NB)).then_inc(s["xnT_ready"], 1)
                link(V.tensor_copy(v4[:, :, 0:8, :], v4[:, :, Q:Q + 8, :]))
                eng.wait_ge(s["silu_done"], k + 1)
                for h in range(H):
                    for b in range(4):
                        t = V.tensor_copy(v4[32 * b:32 * b + 32, h, 8:8 + Q, :],
                                          vF[32 * h:32 * h + 32, :].rearrange("p (n q a) -> p q n a", n=NB, a=4)[:, :, :, b])
                t.then_inc(s["v4_ready"], 1)
                V.transpose(vB[:, :, :], vF[:, :].rearrange("p (g i) -> p g i", g=G))
                eng.wait_ge(s["beta_exp"], k + 1)
                link(V.tensor_scalar(beta[:, :], beta[:, :], 0.5, 0.5, ALU.mult, ALU.add))
                V.transpose(betaB[:, :, :], beta[:, :].rearrange("p (g i) -> p g i", g=G))
                eng.wait_ge(s["ssq_ps"], k + 1)
                link(V.tensor_scalar(rs[:, 0, :], bank(5)[:, 0:2 * A * H], L2_EPS, None, ALU.add))
                inv_sqrt(2 * A * H)
                V.tensor_copy(rs[:, 2, :], rs[:, 1, :]).then_inc(s["rn_ready"], 1)
                eng.wait_ge(s["rnT_ps"], k + 1)
                V.tensor_copy(rnT[:, :], bank(5)[0:2 * A * H, 128:256]).then_inc(s["rnT_ready"], 1)
                eng.wait_ge(s["rnF_ps"], k + 1)
                for i in range(2):
                    t = V.tensor_tensor(kq[:, :, i, :], kqs[:, i, :].rearrange("p (g i) -> p g i", g=G),
                                        bank(6 + i).rearrange("p (g i) -> p g i", g=G), ALU.mult)
                link(t)
                expand(KTbd, kq[:, :, 0, :]).then_inc(s["bd_ready"], 1)
                expand(QTbd, kq[:, :, 1, :])
                link(V.transpose(kB[:, :, :], kq[:, :, 0, :]))
                link(expand(Kbd, kB))
                eng.wait_ge(s["gram_ps"], k + 1)
                gram = bank(1, 2).rearrange("p (g w i) -> p g w i", g=G, w=2)
                V.tensor_tensor(attnT[:, :, :], gram[:, :, 1, :], bc(up), ALU.mult)
                link(V.tensor_tensor(tmpB[:, :, :], gram[:, :, 0, :], bc(low), ALU.mult))
                link(V.tensor_tensor(Lc[:, :, :], tmpB[:, :, :], betaB[:, :, :], ALU.mult))
                link(V.transpose(LT[:, :, :], Lc[:, :, :]))
                link(V.tensor_tensor(M1[:, :, :], Lc[:, :, :], bc(cst[:, C_LEV:C_LEV + 32]), ALU.mult))
                link(V.tensor_tensor(X[:, :, :], bc(eye32), M1[:, :, :], ALU.subtract))
                expand(LTbd, LT).then_inc(s["L_ready"], 1)
                link(V.transpose(XT[:, :, :], X[:, :, :]))
                expand(XTbd, XT).then_inc(s["xt_ready"], 1)
                for l in range(1, LEVELS):
                    lev = cst[:, C_LEV + 32 * l:C_LEV + 32 * l + 32]
                    eng.wait_ge(s["m1_ps"], 4 * k + l)
                    V.tensor_tensor(M1[:, :, :], bank(3).rearrange("p (g i) -> p g i", g=G), bc(lev),
                                    ALU.mult).then_inc(s["m1_ready"], 1)
                    eng.wait_ge(s["m2_ps"], 4 * k + l)
                    link(V.tensor_tensor(X[:, :, :], X[:, :, :], bank(4).rearrange("p (g i) -> p g i", g=G), ALU.subtract))
                    link(V.transpose(XT[:, :, :], X[:, :, :]))
                    if l < LEVELS - 1:
                        expand(XTbd, XT).then_inc(s["xt_ready"], 1)
                link(V.tensor_tensor(XT[:, :, :], XT[:, :, :], betaB[:, :, :], ALU.mult))
                expand(XTbd, XT)
                expand(ATbd, attnT).then_inc(s["scan_ready"], 1)
                for n in range(NCH):
                    m = NCH * k + n
                    eng.wait_ge(s["ks_ps"], m + 1)
                    V.tensor_tensor(r[:, :, :], vB[:, :, :].rearrange("p (b n) i -> p b n i", b=NB)[:, :, n, :],
                                    bank(5)[:, 0:64].rearrange("p (b i) -> p b i", b=NB), ALU.subtract).then_inc(s["r_ready"], 1)
                    eng.wait_ge(s["u_ps"], m + 1)
                    V.tensor_copy(u[:, :, :], bank(6)[:, 0:64].rearrange("p (b i) -> p b i", b=NB)).then_inc(s["u_ready"], 1)
                    eng.wait_ge(s["ds_ps"], m + 1)
                    V.tensor_tensor(S[:, (n + 1) % 2, :, :], S[:, n % 2, :, :],
                                    bank(7)[:, 0:64].rearrange("p (b i) -> p b i", b=NB), ALU.add).then_inc(s["s_ready"], 1)
                eng.wait_ge(s["fir_out"], H * (k + 1))

                def stats(i):
                    return V.tensor_reduce(out=stat[:, :, i, :], in_=SM[:, i, :, :, :], op=ALU.add, axis=AX.X,
                                           apply_absolute_value=True)
                for i in range(4):
                    stats(i)
                eng.wait_ge(s["o_ps"], k + 1)
                link(V.tensor_copy(oB[:, :, :], bank(4).rearrange("p (g i) -> p g i", g=G)))
                V.transpose(oF[:, :].rearrange("p (a q b) -> p b q a", a=A, b=NB),
                            oB[:, :, :].rearrange("p g i -> p (g i)").rearrange("p (b q a) -> p b q a", b=NB, a=A)).then_inc(s["oF_ready"], 1)
                eng.wait_ge(s["tm_out"], 2 * k + 1)
                stats(6)
                eng.wait_ge(s["mix_in"], k + 1)
                stats(4)
                eng.wait_ge(s["tm_out"], 2 * k + 2)
                stats(5).then_inc(s["stat_ready"], 1)
                eng.wait_ge(s["logit_ps"], k + 1)
                V.tensor_tensor(z[:, :, :], bank(3)[:, 0:A * NS * H].rearrange("p (a n) -> p a n", a=A),
                                gb2[:, :, :].rearrange("p s h -> p (s h)").unsqueeze(1).to_broadcast([128, A, NS * H]), ALU.add).then_inc(s["z_ready"], 1)
                eng.wait_ge(s["z_ln"], k + 1)
                link(V.scalar_tensor_tensor(out=z[:, :, :], in0=z[:, :, :], scalar=0.0, in1=zl[:, :, :], op0=ALU.max, op1=ALU.add))
                zf = z[:, :, :].rearrange("p a (s h) -> p a s h", s=NS)
                link(V.tensor_scalar(z[:, :, :], z[:, :, :], GATE_EPS, None, ALU.add))
                link(V.tensor_reduce(out=wsum[:, :, :], in_=z[:, :, :].rearrange("p a (s h) -> p a h s", s=NS), op=ALU.add, axis=AX.X))
                link(V.reciprocal(wsum[:, :, :], wsum[:, :, :]))
                link(V.tensor_tensor(wt[:, :, :, :], zf, wsum[:, :, :].unsqueeze(2).to_broadcast([128, A, NS, H]), ALU.mult))

                def weigh(i, dst):
                    return V.tensor_tensor(dst, SM[:, i, :, :, :],
                                           wt[:, :, i, :].unsqueeze(3).to_broadcast([128, A, H, DH]), ALU.mult)
                weigh(0, acc[:, 0, :, :, :])
                link(weigh(1, prod[:, 1, :, :, :]))
                for i in range(1, NS):
                    t = V.tensor_tensor(acc[:, i % 2, :, :, :], acc[:, (i - 1) % 2, :, :, :], prod[:, i % 2, :, :, :], ALU.add)
                    if i < NS - 1:
                        t = weigh(i + 1, prod[:, (i + 1) % 2, :, :, :])
                    link(t)
                o = acc[:, (NS - 1) % 2, :, :, :]
                pr = prod[:, 0, :, :, :]
                link(V.tensor_tensor(pr, o, o, ALU.mult))
                link(V.tensor_reduce(out=ss[:, :, :], in_=pr, op=ALU.add, axis=AX.X))
                link(V.tensor_scalar(rs[:, 0, 0:A * H], ss[:, :, :].rearrange("p a h -> p (a h)"), 1.0 / DH, RMS_EPS, ALU.mult, ALU.add))
                inv_sqrt(A * H)
                V.tensor_tensor(pr, o, rs[:, 1, 0:A * H].rearrange("p (a h) -> p a h", a=A).unsqueeze(3).to_broadcast([128, A, H, DH]), ALU.mult).then_inc(s["o_ready"], 1)
                eng.wait_ge(s["oT_ps"], k + 1)
                V.tensor_copy(oT[:, :], bank(0)).then_inc(s["oT_ready"], 1)
                eng.wait_ge(s["y_ps"], k + 1)
                link(layer_norm(lambda a: bank(1)[:, 128 * a:128 * a + 128], y1))
                link(V.tensor_tensor(x1[:, :, :], y1[:, :, :], x_all[:, bass.ds(k, 1), :, :].rearrange("p k a d -> p (k a) d"), ALU.add))
                layer_norm(lambda a: x1[:, a, :], x2n).then_inc(s["x2_ready"], 1)
                eng.wait_ge(s["x2T_ps"], k + 1)
                V.tensor_copy(x2T[:, :], bank(0)).then_inc(s["x2T_ready"], 1)
                eng.wait_ge(s["router_ps"], k + 1)
                link(V.tensor_copy(rl[:, :, :], bank(1)[:, 0:A * E].rearrange("p (a e) -> p a e", a=A)))
                carry_wait()
                for a in range(A):
                    t = V.max(top8[:, a, :], rl[:, a, :])
                link(t)
                link(V.tensor_tensor(rrep[:, :, :], rl[:, :, :], top8[:, :, 0:1].to_broadcast([128, A, E]), ALU.subtract))
                V.tensor_copy(want2[:, :, 0:2], top8[:, :, 0:2]).then_inc(s["re_in"], 1)
                link(V.memset(want2[:, :, 2:8], 3.0e38))
                carry_wait()
                for a in range(A):
                    t = V.match_replace(out=cwr[:, 0, a, :], in_to_replace=want2[:, a, :], in_values=rl[:, a, :], imm_value=-3.0e38)
                link(t)
                link(V.tensor_tensor(cwr[:, 1, :, :], rl[:, :, :], cwr[:, 0, :, :], ALU.is_gt))
                eng.wait_ge(s["re_out"], k + 1)
                link(V.tensor_reduce(out=rsum[:, :], in_=re[:, :, :], op=ALU.add, axis=AX.X))
                link(V.reciprocal(rsum[:, :], rsum[:, :]))
                link(V.tensor_tensor(cw[:, :, :], re[:, :, :], cwr[:, 1, :, :], ALU.mult))
                link(V.tensor_tensor(cw[:, :, :], cw[:, :, :], rsum[:, :].unsqueeze(2).to_broadcast([128, A, E]), ALU.mult))
                link(V.tensor_copy(cw3[:, :, 0, :], cw[:, :, :]))
                link(V.tensor_tensor(cwr[:, 0, :, :], cw[:, :, :], cw3[:, :, 0, :], ALU.subtract))
                link(V.tensor_copy(cw3[:, :, 1, :], cwr[:, 0, :, :]))
                link(V.tensor_tensor(cwr[:, 1, :, :], cwr[:, 0, :, :], cw3[:, :, 1, :], ALU.subtract))
                V.tensor_copy(cw3[:, :, 2, :], cwr[:, 1, :, :]).then_inc(s["cw_ready"], 1)
                eng.wait_ge(s["cwT_ps"], k + 1)
                V.tensor_copy(cwT[:, :], bank(0)[0:48, 0:256].bitcast(bf16)).then_inc(s["cwT_ready"], 1)
                for j in range(PAIRS + 1):
                    n = (PAIRS + 1) * k + j
                    p = 3 * (j % 2)
                    eng.wait_ge(s["sg_ready"], n + 1)
                    if j < PAIRS:
                        link(V.tensor_tensor(sc[:, j % 2, :], sg[:, j % 2, :], bank(3 + p), ALU.mult))
                    a_ = sc if j < PAIRS else sg
                    if j >= 2:
                        eng.wait_ge(s["z_ps"], n - 1)
                    V.tensor_tensor(hT[:, j % 2, :], a_[:, j % 2, :], bank(1 + p), ALU.mult).then_inc(s["h_ready"], 1)
                eng.wait_ge(s["z_ps"], (PAIRS + 1) * (k + 1))
                V.tensor_copy(zT[:, :], bank(7)).then_inc(s["zT_ready"], 1)
                eng.wait_ge(s["yo_ps"], k + 1)
                link(layer_norm(lambda a: bank(0)[:, 128 * a:128 * a + 128], y1))
                V.tensor_tensor(x_all[:, bass.ds(k, 1), :, :].rearrange("p k a d -> p (k a) d"), y1[:, :, :], x1[:, :, :], ALU.add).then_inc(s["y_ready"], 1)
                assert cnt[0] == CH, f"DVE_STEPS is {cnt[0]}"

        @block.tensor
        def _(eng):
            T = nc.tensor
            eng.wait_ge(w_in, WTOTAL)
            eng.wait_ge(init, 13)

            def mm(o, lhsT, rhs, start=True, stop=True):
                return T.matmul(o, lhsT, rhs, start=start, stop=stop)

            for i in range(3):
                T.transpose(bank(0)[:, 128 * i:128 * i + 128], wraw[:, i, :], ident)
            T.transpose(bank(0)[:, 384:400], wg_raw[:, :], cst[0:E, 0:E]).then_inc(wprep_pe, 1)
            eng.wait_ge(wprep, 2)
            for i in range(3):
                mm(bank(1 + i), wrawT[:, i, :], diag[:, i, :, :].rearrange("p t n -> p (t n)")).then_inc(wprep_pe, 1)
            eng.wait_ge(wprep, 5)
            eng.wait_ge(toep_ready, 1)

            def transposes(src, cols=128, part=128, idt=ident, dst=None):
                for a in range(A):
                    t = T.transpose((bank(0) if dst is None else dst)[0:cols, 128 * a:128 * a + 128], src(a), idt)
                return t

            with eng.Fori(0, TILES) as k:
                eng.wait_ge(s["xn_ready"], k + 1)
                transposes(lambda a: xn[:, a, :]).then_inc(s["xnT_ps"], 1)
                eng.wait_ge(s["xnT_ready"], k + 1)
                for j, i in enumerate((1, 0, 2)):
                    for tap in range(4):
                        t = mm(bank(1 + j), wtap[:, i, tap, :], xnT[:, :, tap:tap + TB], start=tap == 0, stop=tap == 3)
                t.then_inc(s["qkv_ps"], 1)
                mm(bank(4), wb_rep[:, :, :].rearrange("p h c -> p (h c)"), xnT[:, :, 3:3 + TB]).then_inc(s["beta_ps"], 1)
                eng.wait_ge(s["sq_done"], k + 1)
                for i in range(2):
                    for a in range(A):
                        c = H * (A * i + a)
                        t = mm(bank(5)[:, c:c + H], sq[:, i, 128 * a:128 * a + 128], cst[:, C_ONES:C_ONES + 128:DH])
                t.then_inc(s["ssq_ps"], 1)
                transposes(lambda a: vP[:, 128 * a:128 * a + 128]).then_inc(s["tm_ps"], 1)
                eng.wait_ge(s["rn_ready"], k + 1)
                T.transpose(bank(5)[0:2 * A * H, 128:256], rs[:, 2, :], ident).then_inc(s["rnT_ps"], 1)
                eng.wait_ge(s["rnT_ready"], k + 1)
                for i in range(2):
                    for a in range(A):
                        t = mm(bank(6 + i)[:, 128 * a:128 * a + 128], headsel[:, A * i + a, :], rnT[:, :])
                t.then_inc(s["rnF_ps"], 1)
                eng.wait_ge(s["bd_ready"], k + 1)
                for g in range(G):
                    t = mm(PS[:, 512 + 64 * g:512 + 64 * g + 64], KTbd[:, g, :], kq[:, g, :, :].rearrange("p w i -> p (w i)"))
                t.then_inc(s["gram_ps"], 1)
                eng.wait_ge(s["L_ready"], k + 1)
                for l in range(1, LEVELS):
                    eng.wait_ge(s["xt_ready"], 4 * k + l)
                    for g in range(G):
                        t = mm(bank(3)[:, 32 * g:32 * g + 32], LTbd[:, g, :], X[:, g, :])
                    t.then_inc(s["m1_ps"], 1)
                    eng.wait_ge(s["m1_ready"], 4 * k + l)
                    for g in range(G):
                        t = mm(bank(4)[:, 32 * g:32 * g + 32], XTbd[:, g, :], M1[:, g, :])
                    t.then_inc(s["m2_ps"], 1)
                eng.wait_ge(s["scan_ready"], k + 1)
                eng.wait_ge(s["v4_ready"], k + 1)

                fir = [(h, m) for h in range(H) for m in range(MX)]

                def fir_step(count):
                    for _ in range(count):
                        if not fir:
                            return
                        h, m = fir.pop(0)
                        w = 128 * sum(m < x for x in MS)
                        if m == 0 and h >= 2:
                            eng.wait_ge(s["fir_out"], 4 * k + h - 1)
                        t = mm(bank(1 + h % 2)[:, 0:w], v4[:, h, 8 - m:8 - m + Q, :].rearrange("p q b -> p (q b)"),
                               toep[m][:, h, :, :, :].rearrange("p s a c -> p (s a c)"), start=m == 0, stop=m == MX - 1)
                        if m == MX - 1:
                            t.then_inc(s["fir_ps"], 1)

                for n in range(NCH):
                    sn = NCH * k + n
                    eng.wait_ge(s["s_ready"], sn + 1)
                    gs = [(b, b * NCH + n) for b in range(NB)]
                    for b, g in gs:
                        t = mm(bank(5)[:, 32 * b:32 * b + 32], KTbd[:, g, :], S[:, n % 2, b, :])
                    t.then_inc(s["ks_ps"], 1)
                    fir_step(2)
                    eng.wait_ge(s["r_ready"], sn + 1)
                    for b, g in gs:
                        t = mm(bank(6)[:, 32 * b:32 * b + 32], XTbd[:, g, :], r[:, b, :])
                    t.then_inc(s["u_ps"], 1)
                    fir_step(2)
                    eng.wait_ge(s["u_ready"], sn + 1)
                    for b, g in gs:
                        t = mm(bank(7)[:, 32 * b:32 * b + 32], Kbd[:, g, :], u[:, b, :])
                    t.then_inc(s["ds_ps"], 1)
                    for b, g in gs:
                        mm(bank(4)[:, 32 * g:32 * g + 32], QTbd[:, g, :], S[:, n % 2, b, :], stop=False)
                        t = mm(bank(4)[:, 32 * g:32 * g + 32], ATbd[:, g, :], u[:, b, :], start=False)
                    if n == NCH - 1:
                        t.then_inc(s["o_ps"], 1)
                    fir_step(1)
                fir_step(99)
                eng.wait_ge(s["oF_ready"], k + 1)
                eng.wait_ge(s["tm_out"], 2 * k + 1)
                transposes(lambda a: oF[:, 128 * a:128 * a + 128]).then_inc(s["tm_ps"], 1)
                eng.wait_ge(s["tm_out"], 2 * k + 2)
                eng.wait_ge(s["stat_ready"], k + 1)
                eng.wait_ge(s["fir_out"], 4 * k + 4)
                for i in range(2):
                    mm(bank(1 + i), g1x[:, 128 * i:128 * i + 128], xnT[:, :, 3:3 + TB], stop=False)
                    if i == 0:
                        transposes(lambda a: stat[:, a, :, :].rearrange("p s h -> p (s h)"), cols=NS * H).then_inc(s["statT_ps"], 1)
                eng.wait_ge(s["statT_ready"], k + 1)
                for i in range(2):
                    mm(bank(1 + i), g1s[:, 128 * i:128 * i + 128], statT, start=False).then_inc(s["hid_ps"], 1)
                eng.wait_ge(s["hid_ready"], 2 * k + 2)
                for a in range(A):
                    for i in range(2):
                        t = mm(bank(3)[:, 28 * a:28 * a + 28], hid[:, i, 128 * a:128 * a + 128],
                               g2[:, i, :, :].rearrange("p s h -> p (s h)"), start=i == 0, stop=i == 1)
                t.then_inc(s["logit_ps"], 1)
                eng.wait_ge(s["o_ready"], k + 1)
                transposes(lambda a: prod[:, 0, a, :, :].rearrange("p h c -> p (h c)")).then_inc(s["oT_ps"], 1)
                eng.wait_ge(s["oT_ready"], k + 1)
                for a in range(A):
                    t = mm(bank(1)[:, 128 * a:128 * a + 128], oT[:, 128 * a:128 * a + 128], wo[:, :])
                t.then_inc(s["y_ps"], 1)
                eng.wait_ge(s["x2_ready"], k + 1)
                transposes(lambda a: x2n[:, a, :]).then_inc(s["x2T_ps"], 1)
                eng.wait_ge(s["x2T_ready"], k + 1)
                for a in range(A):
                    t = mm(bank(1)[:, E * a:E * a + E], x2T[:, 128 * a:128 * a + 128], wgT[:, :])
                t.then_inc(s["router_ps"], 1)
                eng.wait_ge(s["cw_ready"], k + 1)
                transposes(lambda a: cw3[:, a, :, :].rearrange("p c e -> p (c e)"), idt=identb[:, :],
                           dst=bank(0)[:, 0:256].bitcast(bf16)).then_inc(s["cwT_ps"], 1)
                eng.wait_ge(s["cwT_ready"], k + 1)

                def up(j):
                    p = 3 * (j % 2)
                    if j >= 2:
                        eng.wait_ge(s["h_ready"], (PAIRS + 1) * k + j - 1)
                    if j < PAIRS:
                        mm(bank(2 + p), w1[:, j, 1, :, :].rearrange("p e h -> p (e h)"), x2T[:, :])
                        mm(bank(1 + p), w1[:, j, 0, :, :].rearrange("p e h -> p (e h)"), x2T[:, :])
                        return mm(bank(3 + p), selb[:, j, :], cwT[:, :])
                    mm(bank(2 + p), ws1[:, HS:2 * HS], x2T[:, :])
                    return mm(bank(1 + p), ws1[:, 0:HS], x2T[:, :])

                up(0).then_inc(s["up_ps"], 1)
                for j in range(PAIRS + 1):
                    if j < PAIRS:
                        up(j + 1).then_inc(s["up_ps"], 1)
                    eng.wait_ge(s["h_ready"], (PAIRS + 1) * k + j + 1)
                    mm(bank(7), w2[:, j, :] if j < PAIRS else ws2[:, :], hT[:, j % 2, :], start=j == 0, stop=j == PAIRS).then_inc(s["z_ps"], 1)
                eng.wait_ge(s["zT_ready"], k + 1)
                transposes(lambda a: zT[:, 128 * a:128 * a + 128]).then_inc(s["yo_ps"], 1)


DVE_STEPS = 159

_INS = ["hidden_states", "w_q", "w_k", "w_v", "w_b", "conv_q_w", "conv_k_w", "conv_v_w", "fir1", "fir3", "fir7",
        "fir15", "fir31", "gate_w1", "gate_b1", "gate_w2", "gate_b2", "norm_w", "w_o"]
_FFN = ["Wg", "W1", "W2", "Ws1", "Ws2"]


def kernel(**inputs):
    import numpy as _np
    import concourse.bacc as _bacc
    from concourse import mybir as _mybir
    from concourse.bass_utils import run_bass_kernel_spmd as _run

    nc = _bacc.Bacc("TRN2", target_bir_lowering=False, num_devices=1)
    arrays, args = {}, []
    for name in ["L0_attn_" + n for n in _INS] + ["L0_ffn_" + n for n in _FFN]:
        arrays[name] = _np.ascontiguousarray(inputs[name])
    arrays["shape_constants"] = shape_constants()
    for name, a in arrays.items():
        args.append(nc.dram_tensor(name, a.shape, _mybir.dt.from_np(a.dtype), kind="ExternalInput").ap())
    out = nc.dram_tensor("out", (NB, SEQ, D), _mybir.dt.float32, kind="ExternalOutput").ap()
    build(nc, *args, out)
    r = _run(nc, [arrays], core_ids=[0])
    return r.results[0]["out"]
```

```python
import concourse.bass as bass
from concourse import mybir
from contextlib import ExitStack
import numpy as np

NB, SEQ, D = 2, 1024, 128
H, DH, C = 4, 32, 32
TILES = 4
TB = SEQ // TILES
TT = NB * TB
NCH = TB // C
G = NB * NCH
A = 4
Q = TB // A
FIRS = (31, 15, 7, 3)
MS = [(k + 3 + 3) // 4 for k in FIRS]
MX = MS[0]
NS = 7
STREAM = (4, 3, 2, 1, 0, 5, 6)
E, HE, HS = 16, 64, 128
PAIRS = E // 2
LN_EPS, L2_EPS, RMS_EPS, GATE_EPS = 1e-5, 1e-6, 1e-5, 0.02
LEVELS = 5

C_ID = 0
C_ONES = 128
C_I32 = 256
C_LOW = 288
C_UP = 320
C_LEV = 352
C_HEAD = 512
C_SEL = 512 + 1024
C_END = C_SEL + PAIRS * 128


def shape_constants():
    c = np.zeros((128, C_END), np.float32)
    p, j, r = np.arange(128)[:, None], np.arange(32)[None, :], np.arange(128)[None, :]
    i = p % 32
    c[:, C_ID:C_ID + 128] = p == r
    c[:, C_ONES:C_ONES + 128] = p // 32 == r // 32
    c[:, C_I32:C_I32 + 32] = i == j
    c[:, C_LOW:C_LOW + 32] = j < i
    c[:, C_UP:C_UP + 32] = i <= j
    for l in range(LEVELS):
        s = 1 << l
        c[:, C_LEV + 32 * l:C_LEV + 32 * l + 32] = (i // (2 * s) == j // (2 * s)) & (i // s % 2 == 1) & (j // s % 2 == 0)
    for t in range(2 * A):
        c[:32, C_HEAD + 128 * t:C_HEAD + 128 * t + 128] = p[:32] == H * t + r // DH
    for t in range(PAIRS):
        c[:48, C_SEL + 128 * t:C_SEL + 128 * t + 128] = (p[:48] % 16) == 2 * t + r // 64
    return c


def build(nc, x_dram, w_q, w_k, w_v, w_b, conv_q, conv_k, conv_v, fir1, fir3, fir7, fir15, fir31,
          gate_w1, gate_b1, gate_w2, gate_b2, norm_w, w_o, Wg, W1, W2, Ws1, Ws2, consts, out):
    f32, bf16 = mybir.dt.float32, mybir.dt.bfloat16
    ALU, ACT, AX = mybir.AluOpType, mybir.ActivationFunctionType, mybir.AxisListType

    ctx = ExitStack()
    with ctx:
        def sb(name, shape, dt=f32):
            return ctx.enter_context(nc.sbuf_tensor(name, shape, dt))

        def sem(name):
            return ctx.enter_context(nc.semaphore(name))

        cst = sb("cst", [128, C_HEAD])
        ident = cst[:, C_ID:C_ID + 128]
        eye32 = cst[:, C_I32:C_I32 + 32]
        low = cst[:, C_LOW:C_LOW + 32]
        up = cst[:, C_UP:C_UP + 32]
        headsel = sb("headsel", [32, 2 * A, 128])
        selb = sb("selb", [48, PAIRS, 128], bf16)
        identb = sb("identb", [128, 128], bf16)
        ffn = sb("ffn", [128, 6, TT])
        sg, sc, hT = ffn[:, 0:2, :], ffn[:, 2:4, :], ffn[:, 4:6, :]
        diag = ffn[:, 0:3, :].rearrange("p i (t n) -> p i t n", t=4)
        wraw = ffn[:, 3, 0:384].rearrange("p (i n) -> p i n", i=3)
        wrawT = ffn[:, 4, 0:384].rearrange("p (i n) -> p i n", i=3)
        convw = sb("convw", [128, 3, 4])
        wtap = sb("wtap", [128, 3, 4, 128])
        wb_raw = sb("wb_raw", [128, H])
        wb_rep = sb("wb_rep", [128, H, 32])
        firw = [sb(f"firw{s}", [128, H, 4 * MS[s]]) for s in range(4)]
        toep = [sb(f"toep{m}", [128, H, sum(m < x for x in MS), A, 32]) for m in range(MX)]
        fir1_row = sb("fir1_row", [128, 128])
        g1x = sb("g1x", [128, 2 * D])
        g1s = sb("g1s", [NS * H, 2 * D])
        gb1 = sb("gb1", [128, 2])
        g2raw = sb("g2raw", [128, 2, NS * H])
        g2 = sb("g2", [128, 2, NS, H])
        gb2raw = sb("gb2raw", [128, NS * H])
        gb2 = sb("gb2", [128, NS, H])
        normw = sb("normw", [128, 1])
        wo_raw = sb("wo_raw", [128, 128])
        sel = sb("sel", [48, PAIRS * 128])
        wo = sb("wo", [128, 128])
        wg_raw = sb("wg_raw", [E, 128])
        wgT = sb("wgT", [128, E])
        w1 = sb("w1", [128, PAIRS, 2, 2, HE])
        w2 = sb("w2", [128, PAIRS, 128])
        ws1 = sb("ws1", [128, 2 * HS])
        ws2 = sb("ws2", [128, 128])
        one = sb("one", [128, 1])

        x_all = sb("x_all", [128, TILES, A, 128])
        st = sb("st", [128, A, 6])
        mv = sb("mv", [128, A, 2])
        rs = sb("rs", [128, 3, 2 * A * H])
        rnT = sb("rnT", [2 * A * H, 128])
        spare = sb("spare", [1, 1])
        xn = sb("xn", [128, A, 128])
        xnT = sb("xnT", [128, NB, 3 + TB])
        kqs = sb("kqs", [128, 2, TT])
        vF = sb("vF", [128, TT])
        vP = sb("vP", [128, TT])
        sq = sb("sq", [128, 2, TT])
        kq = sb("kq", [128, G, 2, C])
        beta = sb("beta", [128, TT])
        betaB = sb("betaB", [128, G, C])
        v4 = sb("v4", [128, H, 8 + Q, NB])
        vB = sb("vB", [128, G, C])
        Lc = sb("Lc", [128, G, C])
        LT = sb("LT", [128, G, C])
        X = sb("X", [128, G, C])
        XT = sb("XT", [128, G, C])
        M1 = sb("M1", [128, G, C])
        tmpB = M1
        kB = sb("kB", [128, G, C])
        attnT = sb("attnT", [128, G, C])
        S = sb("S", [128, 2, NB, DH])
        r = sb("r", [128, NB, DH])
        u = sb("u", [128, NB, DH])
        oB = Lc
        oF = vP
        SM = sb("SM", [128, NS, A, H, DH])
        stat = sb("stat", [128, A, NS, H])
        statT = ffn[0:NS * H, 2, :]
        hid = ffn[:, 0:2, :]
        z = sb("z", [128, A, NS * H])
        za = sb("za", [128, A, NS * H])
        ze = sb("ze", [128, A, NS * H])
        zl = sb("zl", [128, A, NS * H])
        wt = sb("wt", [128, A, NS, H])
        wsum = sb("wsum", [128, A, H])
        prod = hid.rearrange("p i (a h c) -> p i a h c", a=A, h=H)
        acc = ffn[:, 4:6, :].rearrange("p i (a h c) -> p i a h c", a=A, h=H)
        ss = sb("ss", [128, A, H])
        oT = sb("oT", [128, TT])
        y1 = sb("y1", [128, A, 128])
        x1 = sb("x1", [128, A, 128])
        x2n = y1
        x2T = sb("x2T", [128, TT])
        rl = sb("rl", [128, A, E])
        top8 = sb("top8", [128, A, 8])
        want2 = sb("want2", [128, A, 8])
        rrep = sb("rrep", [128, A, E])
        re = sb("re", [128, A, E])
        rsum = sb("rsum", [128, A])
        cw = sb("cw", [128, A, E])
        cwr = sb("cwr", [128, 2, A, E])
        cw3 = sb("cw3", [128, A, 8, E], bf16)
        cwT = sb("cwT", [48, TT], bf16)
        zT = oT

        PS = ctx.enter_context(nc.psum_tensor("PS", [128, 8 * 512], f32))

        def bank(i, n=1):
            return PS[:, 512 * i:512 * (i + n)]

        w_in = sem("w_in")
        w_late = sem("w_late")
        x0_in = sem("x0_in")
        x_in = sem("x_in")
        init = sem("init")
        wprep_pe = sem("wprep_pe")
        wprep = sem("wprep")
        toep_ready = sem("toep_ready")
        dve = sem("dve")
        poolc = sem("poolc")
        names = """xn_ready xnT_ps xnT_ready halo qkv_ps beta_ps kq_silu sq_done silu_done vP_done beta_exp
             v4_halo v4_ready ssq_ps rn_ready rnT_ps rnT_ready rnF_ps kq_ready gram_ps x_ready m1_ps m1_ready
             m2_ps T_ready ks_ps r_ready u_ps u_ready ds_ps s_ready o_ps oF_ready fir_ps fir_out vt_ps vt_out
             dt_ps dt_out mix_in stat_ready statT_ps statT_ready hid_ps hid_ready logit_ps z_ready zabs z_exp
             z_ln mixed oT_ps oT_ready y_ps x2_ready x2T_ps x2T_ready router_ps re_in re_out cw_ready cwT_ps
             cwT_ready gate_ps wts_ps up_ps sg_ready sc_ready h_ready z_ps zT_ready yo_ps y_ready y_stored""".split()
        s = {n: sem(n) for n in names}

        block = ctx.enter_context(nc.Block())

        x_v = x_dram.rearrange("b (t q a) d -> b q t (a d)", t=TILES, a=A)
        o_v = out.rearrange("b (t q a) d -> b q t (a d)", t=TILES, a=A)

        early = [
            (cst[:, :], consts[:, 0:C_HEAD]), (wraw[:, 0, :], w_q), (wraw[:, 1, :], w_k), (wraw[:, 2, :], w_v),
            (convw[:, 0, :], conv_q), (convw[:, 1, :], conv_k), (convw[:, 2, :], conv_v),
            (wb_raw[:, :], w_b), (wg_raw[:, :], Wg),
            (headsel[:, :, :], consts[0:32, C_HEAD:C_SEL].rearrange("p (t n) -> p t n", n=128)),
        ]
        late = [
            (fir1_row[:, :], fir1.rearrange("c k -> (c k)").partition_broadcast(128)),
            (g1x[:, :], gate_w1[0:D, :]),
            (gb1[:, :], gate_b1.rearrange("(a p) -> p a", p=128)),
            (g2raw[:, :, :], gate_w2.rearrange("(a p) n -> p a n", p=128)),
            (gb2raw[:, :], gate_b2.partition_broadcast(128)),
            (wo_raw[:, :], w_o), (sel[:, :], consts[0:48, C_SEL:C_END]),
            (w2[:, :, :], W2.rearrange("(t e) h d -> (e h) t d", e=2)),
            (ws1[:, :], Ws1), (ws2[:, :], Ws2),
        ]
        late += [(g1s[4 * i:4 * i + 4, :], gate_w1[D + 4 * STREAM[i]:D + 4 * STREAM[i] + 4, :]) for i in range(NS)]
        late += [(normw[32 * h:32 * h + 32, :], norm_w.rearrange("(c a) -> c a", a=1)) for h in range(H)]
        late += [(w1[:, :, i, e, :], W1.rearrange("(t e) d (i h) -> i e d t h", e=2, i=2)[i, e]) for i in range(2) for e in range(2)]
        W_IN, W_LATE = 16 * len(early), 16 * len(late)

        @block.gpsimd
        def _(eng):
            eng.memset(S[:, :, :, :], 0.0).then_inc(s["s_ready"], 1)
            eng.memset(xnT[:, :, :], 0.0).then_inc(init, 1)
            eng.memset(v4[:, :, :, :], 0.0).then_inc(init, 1)
            eng.memset(one[:, :], 1.0).then_inc(init, 1)
            eng.memset(cw3[:, :, :, :], 0.0).then_inc(init, 1)
            for i in range(4):
                eng.memset(firw[i][:, :, :], 0.0).then_inc(init, 1)
            eng.wait_ge(init, 8)
            with nc.allow_non_contiguous_dma("short rows of taps"):
                for i, w in enumerate((fir31, fir15, fir7, fir3)):
                    for b in range(4):
                        eng.dma_start(firw[i][32 * b:32 * b + 32, :, 5 - b:5 - b + FIRS[i]],
                                      w.rearrange("(h c) k -> c h k", h=H)).then_inc(poolc, 16)
            eng.wait_ge(poolc, 256)
            eng.wait_ge(w_in, W_IN)
            for m in range(MX):
                for i in range(4):
                    if m < MS[i]:
                        for a in range(A):
                            zp = 4 * MS[i] - 1 - 4 * m - a
                            t = eng.tensor_tensor(
                                out=toep[m][:, :, i, a, :],
                                in0=eye32.unsqueeze(1).to_broadcast([128, H, 32]),
                                in1=firw[i][:, :, zp:zp + 1].to_broadcast([128, H, 32]),
                                op=ALU.mult)
            t.then_inc(toep_ready, 1)
            eng.wait_ge(w_late, W_LATE)
            with eng.Fori(0, TILES) as k:
                eng.wait_ge(s["vt_out"], k + 1)
                eng.tensor_tensor(out=SM[:, 4, :, :, :], in0=SM[:, 6, :, :, :],
                                  in1=fir1_row[:, :].rearrange("p (h c) -> p h c", h=H).unsqueeze(1)
                                  .to_broadcast([128, A, H, DH]), op=ALU.mult).then_inc(s["mix_in"], 1)

        @block.sync
        def _(eng):
            with nc.allow_non_contiguous_dma("weights, once"):
                for dst, src in early:
                    eng.dma_start(dst, src).then_inc(w_in, 16)
                for dst, src in late:
                    eng.dma_start(dst, src).then_inc(w_late, 16)
            with eng.Fori(0, TILES) as k:
                eng.wait_ge(s["y_ready"], k + 1)
                for b in range(NB):
                    eng.dma_start(o_v[b, :, bass.ds(k, 1), :], x_all[b:128:2, bass.ds(k, 1), :, :].rearrange("p k a d -> p (k a) d")).then_inc(s["y_stored"], 16)
            eng.wait_ge(s["y_stored"], 32 * TILES)

        @block.scalar
        def _(eng):
            for t in range(TILES):
                for b in range(NB):
                    eng.dma_start(x_all[b:128:2, t, :, :],
                                  x_v[b, :, t, :]).then_inc(x_in if t else x0_in, 16)
            eng.wait_ge(init, 8)

            def tokens_to_features(k):
                if not isinstance(k, int):
                    eng.wait_ge(s["beta_ps"], k)
                    eng.wait_ge(s["hid_ps"], 2 * k)
                eng.activation(xnT[:, :, 0:3], xnT[:, :, TB:TB + 3], ACT.Copy).then_inc(s["halo"], 1)
                eng.wait_ge(s["xnT_ps"], k + 1)
                eng.wait_ge(s["halo"], k + 1)
                eng.activation(xnT[:, :, 3:3 + TB].rearrange("p b (q a) -> p a q b", a=A),
                               bank(0).rearrange("p (a q b) -> p a q b", a=A, b=NB), ACT.Copy).then_inc(s["xnT_ready"], 1)

            def silus(k):
                eng.wait_ge(s["qkv_ps"], k + 1)
                eng.activation(kqs[:, 0, :], bank(1), ACT.Silu)
                eng.activation(kqs[:, 1, :], bank(2), ACT.Silu).then_inc(s["kq_silu"], 1)
                eng.wait_ge(s["kq_silu"], k + 1)
                eng.activation(sq[:, :, :], kqs[:, :, :], ACT.Square).then_inc(s["sq_done"], 1)
                eng.activation(vF[:, :], bank(3), ACT.Silu).then_inc(s["silu_done"], 1)
                eng.activation(vP[:, :].rearrange("p (a q b) -> p b q a", a=A, b=NB),
                               bank(3).rearrange("p (b q a) -> p b q a", a=A, b=NB), ACT.Silu).then_inc(s["vP_done"], 1)
                eng.wait_ge(s["beta_ps"], k + 1)
                eng.activation(beta[:, :], bank(0), ACT.Tanh, scale=0.5).then_inc(s["beta_exp"], 1)
                eng.activation(v4[:, :, 0:8, :], v4[:, :, Q:Q + 8, :], ACT.Copy).then_inc(s["v4_halo"], 1)
                eng.wait_ge(s["silu_done"], k + 1)
                eng.wait_ge(s["v4_halo"], k + 1)
                for h in range(H):
                    for b in range(4):
                        t = eng.activation(v4[32 * b:32 * b + 32, h, 8:8 + Q, :],
                                           vF[32 * h:32 * h + 32, :].rearrange("p (n q a) -> p q n a", n=NB, a=4)[:, :, :, b],
                                           ACT.Copy)
                t.then_inc(s["v4_ready"], 1)

            def scan_u(k, n):
                eng.wait_ge(s["u_ps"], NCH * k + n + 1)
                eng.activation(u[:, :, :], bank(0)[:, 64:128].rearrange("p (b i) -> p b i", b=NB), ACT.Copy).then_inc(s["u_ready"], 1)

            def fir_out(k, h):
                if h == 0 and not isinstance(k, int):
                    eng.wait_ge(s["mixed"], k)
                eng.wait_ge(s["fir_ps"], 4 * k + h + 1)
                eng.activation(SM[:, 0:4, :, h, :],
                               bank((7, 3)[h % 2]).rearrange("p (s a c) -> p s a c", s=4, a=A),
                               ACT.Copy).then_inc(s["fir_out"], 1)

            def v_stream(k):
                eng.wait_ge(s["vt_ps"], k + 1)
                eng.activation(SM[:, 6, :, :, :].rearrange("p a h c -> p (a h c)"), bank(2), ACT.Copy).then_inc(s["vt_out"], 1)

            def delta_stream(k):
                eng.wait_ge(s["dt_ps"], k + 1)
                eng.activation(SM[:, 5, :, :, :].rearrange("p a h c -> p (a h c)"), bank(3), ACT.Copy).then_inc(s["dt_out"], 1)

            def gate_statistics(k):
                eng.wait_ge(s["statT_ps"], k + 1)
                eng.activation(statT.rearrange("s (b q a) -> s a q b", b=NB, a=A),
                               bank(0)[0:NS * H, :].rearrange("s (a q b) -> s a q b", a=A, b=NB),
                               ACT.Copy, scale=1.0 / DH).then_inc(s["statT_ready"], 1)

            def gate(k):
                for i in range(2):
                    eng.wait_ge(s["hid_ps"], 2 * k + i + 1)
                    eng.activation(hid[:, i, :].rearrange("p (a q b) -> p b q a", a=A, b=NB),
                                   bank(4 + i).rearrange("p (b q a) -> p b q a", a=A, b=NB), ACT.Gelu, bias=gb1[:, i:i + 1]).then_inc(s["hid_ready"], 1)
                eng.wait_ge(s["z_ready"], k + 1)
                eng.activation(za[:, :, :], z[:, :, :], ACT.Abs).then_inc(s["zabs"], 1)
                eng.wait_ge(s["zabs"], k + 1)
                eng.activation(ze[:, :, :], za[:, :, :], ACT.Exp, scale=-1.0).then_inc(s["z_exp"], 1)
                eng.wait_ge(s["z_exp"], k + 1)
                eng.activation(zl[:, :, :], ze[:, :, :], ACT.Ln, bias=one[:, :]).then_inc(s["z_ln"], 1)

            def o_features(k):
                eng.wait_ge(s["oT_ps"], k + 1)
                eng.activation(oT[:, :], bank(6), ACT.Copy).then_inc(s["oT_ready"], 1)

            def x2_features(k):
                eng.wait_ge(s["x2T_ps"], k + 1)
                eng.activation(x2T[:, :], bank(6), ACT.Copy).then_inc(s["x2T_ready"], 1)

            def router_exp(k):
                eng.wait_ge(s["re_in"], k + 1)
                eng.activation(re[:, :, :], rrep[:, :, :], ACT.Exp).then_inc(s["re_out"], 1)

            def expert(k, j):
                n = (PAIRS + 1) * k + j
                eng.wait_ge(s["gate_ps"], n + 1)
                if j >= 2:
                    eng.wait_ge(s["h_ready"], n - 1)
                eng.activation(sg[:, j % 2, :], bank(5), ACT.Silu).then_inc(s["sg_ready"], 1)

            def z_features(k):
                eng.wait_ge(s["z_ps"], (PAIRS + 1) * (k + 1))
                eng.activation(zT[:, :], bank(7), ACT.Copy).then_inc(s["zT_ready"], 1)

            def tile(one_, two):
                if two is not None:
                    gate_statistics(two)
                    gate(two)
                if one_ is not None:
                    tokens_to_features(one_)
                    silus(one_)
                if two is not None:
                    o_features(two)
                if one_ is not None:
                    for h in range(3):
                        fir_out(one_, h)
                if two is not None:
                    x2_features(two)
                    expert(two, 0)
                if one_ is not None:
                    fir_out(one_, 3)
                if two is not None:
                    router_exp(two)
                if one_ is not None:
                    v_stream(one_)
                for n in range(NCH):
                    if one_ is not None:
                        scan_u(one_, n)
                    if two is not None:
                        expert(two, n + 1)
                if two is not None:
                    z_features(two)
                if one_ is not None:
                    delta_stream(one_)

            tile(0, None)
            eng.wait_ge(w_late, W_LATE)
            with eng.Fori(1, TILES) as k:
                tile(k, k - 1)
            tile(None, TILES - 1)

        @block.vector
        def _(eng):
            cnt = [0]
            base = [0]

            def carry_wait():
                V.memset(spare[0:1, 0:1], 0.0)

            def link(ins):
                cnt[0] += 1
                ins.then_inc(dve, 1)
                eng.wait_ge(dve, base[0] + cnt[0])

            V = nc.vector

            def bc(ap, n=G):
                return ap.unsqueeze(1).to_broadcast([128, n, 32])

            def inv_sqrt(n):
                v, y, t = rs[:, 0, 0:n], rs[:, 1, 0:n], rs[:, 2, 0:n]
                i32 = mybir.dt.int32
                link(V.tensor_scalar(y.bitcast(i32), v.bitcast(i32), 1, None, ALU.logical_shift_right))
                link(V.tensor_scalar(y.bitcast(i32), y.bitcast(i32), -1.0, float(0x5F3759DF), ALU.mult, ALU.add))
                for _ in range(3):
                    link(V.tensor_tensor(t, y, y, ALU.mult))
                    link(V.scalar_tensor_tensor(out=t, in0=t, scalar=-0.5, in1=v, op0=ALU.mult, op1=ALU.mult))
                    link(V.scalar_tensor_tensor(out=y, in0=t, scalar=1.5, in1=y, op0=ALU.add, op1=ALU.mult))

            def layer_norm(src, dst, ready=None, eps_=LN_EPS):
                for a in range(A):
                    t = V.bn_stats(st[:, a, :], src(a))
                link(t)
                carry_wait()
                for a in range(A):
                    t = V.bn_aggr(mv[:, a, :], st[:, a, :])
                link(t)
                link(V.tensor_scalar(rs[:, 0, 0:A], mv[:, :, 1], eps_, None, ALU.add))
                inv_sqrt(A)
                for a in range(A):
                    t = V.tensor_scalar(dst[:, a, :], src(a), mv[:, a, 0:1], rs[:, 1, a:a + 1],
                                        ALU.subtract, ALU.mult)
                if ready is not None:
                    t.then_inc(ready, 1)
                return t

            eng.wait_ge(w_in, W_IN)
            eng.wait_ge(init, 8)
            V.tensor_copy(identb[:, :], ident)
            V.tensor_copy(wb_rep[:, :, :], wb_raw[:, :].unsqueeze(2).to_broadcast([128, H, 32]))
            for i in range(3):
                for t in range(4):
                    last = V.tensor_scalar(diag[:, i, t, :], ident, convw[:, i, t:t + 1], None, ALU.mult)
            last.then_inc(wprep, 1)
            eng.wait_ge(wprep_pe, 1)
            V.tensor_copy(wrawT[:, :, :], bank(0)[:, 0:384].rearrange("p (i n) -> p i n", i=3))
            V.tensor_copy(wgT[:, :], bank(0)[:, 384:400]).then_inc(wprep, 1)
            for i in range(3):
                eng.wait_ge(wprep_pe, 2 + i)
                V.tensor_copy(wtap[:, i, :, :], bank(1 + i).rearrange("p (t n) -> p t n", t=4)).then_inc(wprep, 1)

            def late_weights():
                eng.wait_ge(w_late, W_LATE)
                V.tensor_copy(selb[:, :, :], sel[:, :].rearrange("e (t p) -> e t p", t=PAIRS))
                V.tensor_scalar(wo[:, :], wo_raw[:, :], normw[:, 0:1], None, ALU.mult)
                for i in range(NS):
                    V.tensor_copy(gb2[:, i, :], gb2raw[:, STREAM[i]::NS])
                for i in range(NS):
                    t = V.tensor_copy(g2[:, :, i, :], g2raw[:, :, STREAM[i]::NS])
                t.then_inc(wprep, 1)

            def feature_groups(ap):
                return ap.rearrange("p (g i) -> p g i", g=G)

            def norm_x(k):
                xk = lambda a: x_all[:, bass.ds(k, 1), a, :].rearrange("p k d -> p (k d)")
                layer_norm(xk, xn, s["xn_ready"])

            def values_and_beta(k):
                eng.wait_ge(s["silu_done"], k + 1)
                V.transpose(vB[:, :, :], feature_groups(vF[:, :]))
                eng.wait_ge(s["beta_exp"], k + 1)
                link(V.tensor_scalar(beta[:, :], beta[:, :], 0.5, 0.5, ALU.mult, ALU.add))
                V.transpose(betaB[:, :, :], feature_groups(beta[:, :]))

            def inverse_norms(k):
                eng.wait_ge(s["ssq_ps"], k + 1)
                link(V.tensor_scalar(rs[:, 0, :], bank(1)[:, 0:2 * A * H], L2_EPS, None, ALU.add))
                inv_sqrt(2 * A * H)
                V.tensor_copy(rs[:, 2, :], rs[:, 1, :]).then_inc(s["rn_ready"], 1)
                eng.wait_ge(s["rnT_ps"], k + 1)
                V.tensor_copy(rnT[:, :], bank(1)[0:2 * A * H, 128:256]).then_inc(s["rnT_ready"], 1)

            def normalise(k):
                eng.wait_ge(s["rnF_ps"], k + 1)
                for i in range(2):
                    t = V.tensor_tensor(kq[:, :, i, :], feature_groups(kqs[:, i, :]), feature_groups(bank(1 + i)), ALU.mult)
                link(t)
                V.transpose(kB[:, :, :], kq[:, :, 0, :]).then_inc(s["kq_ready"], 1)

            def gram_out(k):
                eng.wait_ge(s["gram_ps"], k + 1)
                for f in range(2):
                    gram = bank(1 + f).rearrange("p (g w i) -> p g w i", g=G // 2, w=2)
                    gs = slice(8 * f, 8 * f + 8)
                    V.tensor_tensor(attnT[:, gs, :], gram[:, :, 1, :], bc(up, 8), ALU.mult)
                    t = V.tensor_tensor(tmpB[:, gs, :], gram[:, :, 0, :], bc(low, 8), ALU.mult)
                link(t)
                link(V.tensor_tensor(Lc[:, :, :], tmpB[:, :, :], betaB[:, :, :], ALU.mult))
                link(V.transpose(LT[:, :, :], Lc[:, :, :]))
                link(V.tensor_tensor(M1[:, :, :], Lc[:, :, :], bc(cst[:, C_LEV:C_LEV + 32]), ALU.mult))
                V.tensor_tensor(X[:, :, :], bc(eye32), M1[:, :, :], ALU.subtract).then_inc(s["x_ready"], 2)
                eng.wait_ge(s["x_ready"], 10 * k + 2)
                V.transpose(XT[:, :, :], X[:, :, :])

            def level_a(k, l):
                lev = cst[:, C_LEV + 32 * l:C_LEV + 32 * l + 32]
                for f in range(2):
                    eng.wait_ge(s["m1_ps"], 8 * k + 2 * (l - 1) + f + 1)
                    V.tensor_tensor(M1[:, 8 * f:8 * f + 8, :], bank(1 + f)[:, 0:256].rearrange("p (g i) -> p g i", g=8),
                                    bc(lev, 8), ALU.mult).then_inc(s["m1_ready"], 1)

            def level_b(k, l):
                for f in range(2):
                    gs = slice(8 * f, 8 * f + 8)
                    eng.wait_ge(s["m2_ps"], 8 * k + 2 * (l - 1) + f + 1)
                    V.tensor_tensor(X[:, gs, :], X[:, gs, :], bank(1 + f)[:, 256:512].rearrange("p (g i) -> p g i", g=8),
                                    ALU.subtract).then_inc(s["x_ready"], 1)
                    eng.wait_ge(s["x_ready"], 10 * k + 2 * l + f + 1)
                    if l < LEVELS - 1:
                        V.transpose(XT[:, gs, :], X[:, gs, :])
                    else:
                        link(V.transpose(XT[:, gs, :], X[:, gs, :]))
                        V.tensor_tensor(XT[:, gs, :], XT[:, gs, :], betaB[:, gs, :], ALU.mult).then_inc(s["T_ready"], 1)

            def scan_r(k, n):
                eng.wait_ge(s["ks_ps"], NCH * k + n + 1)
                V.tensor_tensor(r[:, :, :], vB[:, :, :].rearrange("p (b n) i -> p b n i", b=NB)[:, :, n, :],
                                bank(0)[:, 0:64].rearrange("p (b i) -> p b i", b=NB), ALU.subtract).then_inc(s["r_ready"], 1)

            def scan_s(k, n):
                eng.wait_ge(s["ds_ps"], NCH * k + n + 1)
                V.tensor_tensor(S[:, (n + 1) % 2, :, :], S[:, n % 2, :, :],
                                bank(0)[:, 128:192].rearrange("p (b i) -> p b i", b=NB), ALU.add).then_inc(s["s_ready"], 1)

            def stats(i):
                return V.tensor_reduce(out=stat[:, :, i, :], in_=SM[:, i, :, :, :], op=ALU.add, axis=AX.X,
                                       apply_absolute_value=True)

            def delta_out(k):
                eng.wait_ge(s["o_ps"], k + 1)
                link(V.tensor_copy(oB[:, :, :], feature_groups(bank(3))))
                eng.wait_ge(s["vt_ps"], k + 1)
                V.transpose(oF[:, :].rearrange("p (a q b) -> p b q a", a=A, b=NB),
                            oB[:, :, :].rearrange("p g i -> p (g i)").rearrange("p (b q a) -> p b q a", b=NB, a=A)).then_inc(s["oF_ready"], 1)

            def statistics(k, n):
                if n == 0:
                    eng.wait_ge(s["fir_out"], H * (k + 1))
                if n < 4:
                    stats(n)
                elif n == 4:
                    eng.wait_ge(s["vt_out"], k + 1)
                    stats(6)
                elif n == 5:
                    eng.wait_ge(s["mix_in"], k + 1)
                    stats(4)

            def delta_statistics(k):
                eng.wait_ge(s["dt_out"], k + 1)
                stats(5).then_inc(s["stat_ready"], 1)

            def logits_out(k):
                eng.wait_ge(s["logit_ps"], k + 1)
                V.tensor_tensor(z[:, :, :], bank(7)[:, 0:A * NS * H].rearrange("p (a n) -> p a n", a=A),
                                gb2[:, :, :].rearrange("p s h -> p (s h)").unsqueeze(1).to_broadcast([128, A, NS * H]), ALU.add).then_inc(s["z_ready"], 1)

            def mix(k):
                eng.wait_ge(s["z_ln"], k + 1)
                link(V.scalar_tensor_tensor(out=z[:, :, :], in0=z[:, :, :], scalar=0.0, in1=zl[:, :, :], op0=ALU.max, op1=ALU.add))
                zf = z[:, :, :].rearrange("p a (s h) -> p a s h", s=NS)
                link(V.tensor_scalar(z[:, :, :], z[:, :, :], GATE_EPS, None, ALU.add))
                link(V.tensor_reduce(out=wsum[:, :, :], in_=z[:, :, :].rearrange("p a (s h) -> p a h s", s=NS), op=ALU.add, axis=AX.X))
                link(V.reciprocal(wsum[:, :, :], wsum[:, :, :]))
                link(V.tensor_tensor(wt[:, :, :, :], zf, wsum[:, :, :].unsqueeze(2).to_broadcast([128, A, NS, H]), ALU.mult))

                def weigh(i, dst):
                    return V.tensor_tensor(dst, SM[:, i, :, :, :],
                                           wt[:, :, i, :].unsqueeze(3).to_broadcast([128, A, H, DH]), ALU.mult)
                weigh(0, acc[:, 0, :, :, :])
                link(weigh(1, prod[:, 1, :, :, :]))
                for i in range(1, NS):
                    t = V.tensor_tensor(acc[:, i % 2, :, :, :], acc[:, (i - 1) % 2, :, :, :], prod[:, i % 2, :, :, :], ALU.add)
                    if i < NS - 1:
                        t = weigh(i + 1, prod[:, (i + 1) % 2, :, :, :])
                    link(t)
                o = acc[:, (NS - 1) % 2, :, :, :]
                pr = prod[:, 0, :, :, :]
                link(V.tensor_tensor(pr, o, o, ALU.mult))
                link(V.tensor_reduce(out=ss[:, :, :], in_=pr, op=ALU.add, axis=AX.X))
                link(V.tensor_scalar(rs[:, 0, 0:A * H], ss[:, :, :].rearrange("p a h -> p (a h)"), 1.0 / DH, RMS_EPS, ALU.mult, ALU.add))
                inv_sqrt(A * H)
                V.tensor_tensor(pr, o, rs[:, 1, 0:A * H].rearrange("p (a h) -> p a h", a=A).unsqueeze(3).to_broadcast([128, A, H, DH]), ALU.mult).then_inc(s["mixed"], 1)

            def residual(k):
                eng.wait_ge(s["y_ps"], k + 1)
                link(layer_norm(lambda a: bank(4)[:, 128 * a:128 * a + 128], y1))
                link(V.tensor_tensor(x1[:, :, :], y1[:, :, :], x_all[:, bass.ds(k, 1), :, :].rearrange("p k a d -> p (k a) d"), ALU.add))
                layer_norm(lambda a: x1[:, a, :], x2n, s["x2_ready"])

            def router(k):
                eng.wait_ge(s["router_ps"], k + 1)
                link(V.tensor_copy(rl[:, :, :], bank(6)[:, 0:A * E].rearrange("p (a e) -> p a e", a=A)))
                carry_wait()
                for a in range(A):
                    t = V.max(top8[:, a, :], rl[:, a, :])
                link(t)
                V.tensor_tensor(rrep[:, :, :], rl[:, :, :], top8[:, :, 0:1].to_broadcast([128, A, E]), ALU.subtract).then_inc(s["re_in"], 1)
                V.tensor_copy(want2[:, :, 0:2], top8[:, :, 0:2])
                link(V.memset(want2[:, :, 2:8], 3.0e38))
                carry_wait()
                for a in range(A):
                    t = V.match_replace(out=cwr[:, 0, a, :], in_to_replace=want2[:, a, :], in_values=rl[:, a, :], imm_value=-3.0e38)
                link(t)
                link(V.tensor_tensor(cwr[:, 1, :, :], rl[:, :, :], cwr[:, 0, :, :], ALU.is_gt))
                eng.wait_ge(s["re_out"], k + 1)
                link(V.tensor_reduce(out=rsum[:, :], in_=re[:, :, :], op=ALU.add, axis=AX.X))
                link(V.reciprocal(rsum[:, :], rsum[:, :]))
                link(V.tensor_tensor(cw[:, :, :], re[:, :, :], cwr[:, 1, :, :], ALU.mult))
                link(V.tensor_tensor(cw[:, :, :], cw[:, :, :], rsum[:, :].unsqueeze(2).to_broadcast([128, A, E]), ALU.mult))
                link(V.tensor_copy(cw3[:, :, 0, :], cw[:, :, :]))
                link(V.tensor_tensor(cwr[:, 0, :, :], cw[:, :, :], cw3[:, :, 0, :], ALU.subtract))
                link(V.tensor_copy(cw3[:, :, 1, :], cwr[:, 0, :, :]))
                link(V.tensor_tensor(cwr[:, 1, :, :], cwr[:, 0, :, :], cw3[:, :, 1, :], ALU.subtract))
                V.tensor_copy(cw3[:, :, 2, :], cwr[:, 1, :, :]).then_inc(s["cw_ready"], 1)
                eng.wait_ge(s["cwT_ps"], k + 1)
                V.tensor_copy(cwT[:, :], bank(6)[0:48, 0:256].bitcast(bf16)).then_inc(s["cwT_ready"], 1)

            def weigh_expert(k, j):
                eng.wait_ge(s["sg_ready"], (PAIRS + 1) * k + j + 1)
                if j > 0:
                    eng.wait_ge(s["wts_ps"], PAIRS * k + j)
                    V.tensor_tensor(sc[:, j % 2, :], sg[:, j % 2, :], bank(6), ALU.mult).then_inc(s["sc_ready"], 1)

            def expert_hidden(k, j):
                n = (PAIRS + 1) * k + j
                if j > 0:
                    eng.wait_ge(s["sc_ready"], PAIRS * k + j)
                eng.wait_ge(s["up_ps"], n + 1)
                a_ = sc if j > 0 else sg
                if j >= 2:
                    carry_wait()
                    eng.wait_ge(s["z_ps"], n - 1)
                V.tensor_tensor(hT[:, j % 2, :], a_[:, j % 2, :], bank(4), ALU.mult).then_inc(s["h_ready"], 1)

            def result(k):
                eng.wait_ge(s["yo_ps"], k + 1)
                link(layer_norm(lambda a: bank(6)[:, 128 * a:128 * a + 128], y1))
                V.tensor_tensor(x_all[:, bass.ds(k, 1), :, :].rearrange("p k a d -> p (k a) d"), y1[:, :, :], x1[:, :, :], ALU.add).then_inc(s["y_ready"], 1)

            def tile(at, one_, two):
                base[0], cnt[0] = at, 0
                if one_ is not None:
                    norm_x(one_)
                if two is not None:
                    logits_out(two)
                    mix(two)
                if one_ is not None:
                    values_and_beta(one_)
                    inverse_norms(one_)
                if two is not None:
                    residual(two)
                if one_ is not None:
                    normalise(one_)
                if two is not None:
                    weigh_expert(two, 0)
                    expert_hidden(two, 0)
                    router(two)
                if one_ is not None:
                    gram_out(one_)
                    for l in range(1, LEVELS):
                        level_a(one_, l)
                        level_b(one_, l)
                for n in range(NCH):
                    if one_ is not None:
                        scan_r(one_, n)
                    if two is not None:
                        weigh_expert(two, n + 1)
                    if one_ is not None:
                        scan_s(one_, n)
                    if two is not None:
                        expert_hidden(two, n + 1)
                    if one_ is not None:
                        statistics(one_, n)
                if one_ is not None:
                    delta_out(one_)
                    delta_statistics(one_)
                if two is not None:
                    result(two)
                return cnt[0]

            eng.wait_ge(x0_in, 32)
            at = tile(0, 0, None)
            late_weights()
            eng.wait_ge(x_in, 32 * (TILES - 1))
            with eng.Fori(1, TILES) as k:
                assert tile(at + LOOP_STEPS * (k - 1), k, k - 1) == LOOP_STEPS, f"LOOP_STEPS is {cnt[0]}"
            tile(at + LOOP_STEPS * (TILES - 1), None, TILES - 1)

        @block.tensor
        def _(eng):
            T = nc.tensor
            eng.wait_ge(w_in, W_IN)
            eng.wait_ge(init, 8)

            def mm(o, lhsT, rhs, start=True, stop=True):
                return T.matmul(o, lhsT, rhs, start=start, stop=stop)

            for i in range(3):
                T.transpose(bank(0)[:, 128 * i:128 * i + 128], wraw[:, i, :], ident)
            T.transpose(bank(0)[:, 384:400], wg_raw[:, :], cst[0:E, 0:E]).then_inc(wprep_pe, 1)
            eng.wait_ge(wprep, 2)
            for i in range(3):
                mm(bank(1 + i), wrawT[:, i, :], diag[:, i, :, :].rearrange("p t n -> p (t n)")).then_inc(wprep_pe, 1)
            eng.wait_ge(wprep, 5)

            def carry_wait():
                T.matmul(bank(0)[:, 448:480], identb[:, :], identb[:, 0:32], start=True, stop=True)

            def mm4(o, lhsT, rhs, start=True, stop=True):
                for h in range(H):
                    q = slice(32 * h, 32 * h + 32)
                    t = T.matmul(o[q, :], lhsT[q, :], rhs[q, :], start=start, stop=stop, tile_position=(32 * h, 32 * h))
                return t

            def transposes(n, src, cols=128):
                for a in range(A):
                    t = T.transpose(bank(n)[0:cols, 128 * a:128 * a + 128], src(a), ident)
                return t

            def flat(ap):
                return ap.rearrange("p h c -> p (h c)")

            def x_transposes(k):
                eng.wait_ge(s["xn_ready"], k + 1)
                transposes(0, lambda a: xn[:, a, :]).then_inc(s["xnT_ps"], 1)

            def projections(k):
                eng.wait_ge(s["xnT_ready"], k + 1)
                if not isinstance(k, int):
                    eng.wait_ge(s["vt_out"], k)
                    eng.wait_ge(s["dt_out"], k)
                for j, i in enumerate((1, 0, 2)):
                    for tap in range(4):
                        t = mm(bank(1 + j), wtap[:, i, tap, :], xnT[:, :, tap:tap + TB], start=tap == 0, stop=tap == 3)
                t.then_inc(s["qkv_ps"], 1)
                mm(bank(0), flat(wb_rep[:, :, :]), xnT[:, :, 3:3 + TB]).then_inc(s["beta_ps"], 1)

            def square_sums(k):
                eng.wait_ge(s["sq_done"], k + 1)
                for i in range(2):
                    for a in range(A):
                        c = H * (A * i + a)
                        t = mm(bank(1)[:, c:c + H], sq[:, i, 128 * a:128 * a + 128], cst[:, C_ONES:C_ONES + 128:DH])
                t.then_inc(s["ssq_ps"], 1)

            def norm_rows(k):
                eng.wait_ge(s["rn_ready"], k + 1)
                T.transpose(bank(1)[0:2 * A * H, 128:256], rs[:, 2, :], ident).then_inc(s["rnT_ps"], 1)
                eng.wait_ge(s["vP_done"], k + 1)
                eng.wait_ge(s["rnT_ready"], k + 1)
                for i in range(2):
                    for a in range(A):
                        t = mm(bank(1 + i)[:, 128 * a:128 * a + 128], headsel[:, A * i + a, :], rnT[:, :])
                t.then_inc(s["rnF_ps"], 1)

            def grams(k):
                eng.wait_ge(s["kq_ready"], k + 1)
                carry_wait()
                for g in range(G):
                    t = mm4(PS[:, 512 + 64 * g:512 + 64 * g + 64], kq[:, g, 0, :], kq[:, g, :, :].rearrange("p w i -> p (w i)"))
                t.then_inc(s["gram_ps"], 1)

            def level_a(k, l):
                for f in range(2):
                    eng.wait_ge(s["x_ready"], 10 * k + 2 * (l - 1) + f + 1)
                    carry_wait()
                    for g in range(8):
                        t = mm4(bank(1 + f)[:, 32 * g:32 * g + 32], LT[:, 8 * f + g, :], X[:, 8 * f + g, :])
                    t.then_inc(s["m1_ps"], 1)

            def level_b(k, l):
                for f in range(2):
                    eng.wait_ge(s["m1_ready"], 8 * k + 2 * (l - 1) + f + 1)
                    carry_wait()
                    for g in range(8):
                        t = mm4(bank(1 + f)[:, 256 + 32 * g:256 + 32 * g + 32], XT[:, 8 * f + g, :], M1[:, 8 * f + g, :])
                    t.then_inc(s["m2_ps"], 1)

            def fir(k, h):
                if h == 0 and not isinstance(k, int):
                    eng.wait_ge(s["z_ready"], k)
                if h == 0:
                    eng.wait_ge(s["v4_ready"], k + 1)
                if h == 0 and isinstance(k, int):
                    eng.wait_ge(toep_ready, 1)
                if h >= 2:
                    eng.wait_ge(s["fir_out"], H * k + h - 1)
                for m in range(MX):
                    w = 128 * sum(m < x for x in MS)
                    t = mm(bank((7, 3)[h % 2])[:, 0:w], v4[:, h, 8 - m:8 - m + Q, :].rearrange("p q b -> p (q b)"),
                           toep[m][:, h, :, :, :].rearrange("p s a c -> p (s a c)"), start=m == 0, stop=m == MX - 1)
                t.then_inc(s["fir_ps"], 1)

            def scan(k, n, filler):
                sn = NCH * k + n
                eng.wait_ge(s["s_ready"], sn + 1)
                gs = [(b, b * NCH + n) for b in range(NB)]
                carry_wait()
                for b, g in gs:
                    t = mm4(bank(0)[:, 32 * b:32 * b + 32], kq[:, g, 0, :], S[:, n % 2, b, :])
                t.then_inc(s["ks_ps"], 1)
                filler(0)
                eng.wait_ge(s["r_ready"], sn + 1)
                carry_wait()
                for b, g in gs:
                    t = mm4(bank(0)[:, 64 + 32 * b:96 + 32 * b], XT[:, g, :], r[:, b, :])
                t.then_inc(s["u_ps"], 1)
                filler(1)
                eng.wait_ge(s["u_ready"], sn + 1)
                carry_wait()
                for b, g in gs:
                    t = mm4(bank(0)[:, 128 + 32 * b:160 + 32 * b], kB[:, g, :], u[:, b, :])
                t.then_inc(s["ds_ps"], 1)
                for b, g in gs:
                    mm4(bank(3)[:, 32 * g:32 * g + 32], kq[:, g, 1, :], S[:, n % 2, b, :], stop=False)
                    t = mm4(bank(3)[:, 32 * g:32 * g + 32], attnT[:, g, :], u[:, b, :], start=False)
                if n == NCH - 1:
                    t.then_inc(s["o_ps"], 1)
                filler(2)

            def v_tokens(k):
                transposes(2, lambda a: vP[:, 128 * a:128 * a + 128]).then_inc(s["vt_ps"], 1)

            def delta_tokens(k):
                eng.wait_ge(s["oF_ready"], k + 1)
                transposes(3, lambda a: oF[:, 128 * a:128 * a + 128]).then_inc(s["dt_ps"], 1)

            def hidden(k):
                for i in range(2):
                    mm(bank(4 + i), g1x[:, 128 * i:128 * i + 128], xnT[:, :, 3:3 + TB], stop=False)
                eng.wait_ge(s["stat_ready"], k + 1)
                T.matmul(bank(0)[:, 0:32], ident, ident[:, 0:32], start=True, stop=True)
                transposes(0, lambda a: stat[:, a, :, :].rearrange("p s h -> p (s h)"), cols=NS * H).then_inc(s["statT_ps"], 1)
                eng.wait_ge(s["statT_ready"], k + 1)
                for i in range(2):
                    mm(bank(4 + i), g1s[:, 128 * i:128 * i + 128], statT, start=False).then_inc(s["hid_ps"], 1)

            def logits(k):
                eng.wait_ge(s["hid_ready"], 2 * k + 2)
                for a in range(A):
                    for i in range(2):
                        t = mm(bank(7)[:, 28 * a:28 * a + 28], hid[:, i, 128 * a:128 * a + 128],
                               g2[:, i, :, :].rearrange("p s h -> p (s h)"), start=i == 0, stop=i == 1)
                t.then_inc(s["logit_ps"], 1)

            def output_projection(k):
                eng.wait_ge(s["mixed"], k + 1)
                transposes(6, lambda a: flat(prod[:, 0, a, :, :])).then_inc(s["oT_ps"], 1)
                eng.wait_ge(s["oT_ready"], k + 1)
                for a in range(A):
                    t = mm(bank(4)[:, 128 * a:128 * a + 128], oT[:, 128 * a:128 * a + 128], wo[:, :])
                t.then_inc(s["y_ps"], 1)

            def router(k):
                eng.wait_ge(s["x2_ready"], k + 1)
                transposes(6, lambda a: x2n[:, a, :]).then_inc(s["x2T_ps"], 1)
                eng.wait_ge(s["x2T_ready"], k + 1)
                for a in range(A):
                    t = mm(bank(6)[:, E * a:E * a + E], x2T[:, 128 * a:128 * a + 128], wgT[:, :])
                t.then_inc(s["router_ps"], 1)

            def router_weights(k):
                eng.wait_ge(s["cw_ready"], k + 1)
                for a in range(A):
                    t = T.transpose(bank(6)[:, 0:256].bitcast(bf16)[:, 128 * a:128 * a + 128],
                                    cw3[:, a, :, :].rearrange("p c e -> p (c e)"), identb[:, :])
                t.then_inc(s["cwT_ps"], 1)
                eng.wait_ge(s["cwT_ready"], k + 1)

            def expert_gate(k, j):
                if j > 0:
                    eng.wait_ge(s["sg_ready"], (PAIRS + 1) * k + j)
                mm(bank(5), flat(w1[:, j - 1, 1, :, :]) if j else ws1[:, HS:2 * HS], x2T[:, :]).then_inc(s["gate_ps"], 1)

            def expert_weights(k, j):
                if j > 1:
                    eng.wait_ge(s["sc_ready"], PAIRS * k + j - 1)
                mm(bank(6), selb[:, j - 1, :], cwT[:, :]).then_inc(s["wts_ps"], 1)

            def expert_up(k, j):
                if j > 0:
                    eng.wait_ge(s["h_ready"], (PAIRS + 1) * k + j)
                mm(bank(4), flat(w1[:, j - 1, 0, :, :]) if j else ws1[:, 0:HS], x2T[:, :]).then_inc(s["up_ps"], 1)

            def expert_down(k, j):
                eng.wait_ge(s["h_ready"], (PAIRS + 1) * k + j + 1)
                mm(bank(7), w2[:, j - 1, :] if j else ws2[:, :], hT[:, j % 2, :],
                   start=j == 0, stop=j == PAIRS).then_inc(s["z_ps"], 1)

            def expert_tokens(k):
                eng.wait_ge(s["zT_ready"], k + 1)
                transposes(6, lambda a: zT[:, 128 * a:128 * a + 128]).then_inc(s["yo_ps"], 1)

            def tile(one_, two):
                if two is not None:
                    hidden(two)
                    logits(two)
                if one_ is not None:
                    x_transposes(one_)
                    projections(one_)
                    square_sums(one_)
                    fir(one_, 0)
                    fir(one_, 1)
                if two is not None:
                    output_projection(two)
                if one_ is not None:
                    norm_rows(one_)
                    fir(one_, 2)
                if two is not None:
                    router(two)
                    expert_gate(two, 0)
                    expert_up(two, 0)
                if one_ is not None:
                    fir(one_, 3)
                if two is not None:
                    router_weights(two)
                if one_ is not None:
                    grams(one_)
                    for l in range(1, LEVELS):
                        level_a(one_, l)
                        level_b(one_, l)
                    eng.wait_ge(s["T_ready"], 2 * one_ + 2)
                    eng.wait_ge(s["fir_out"], H * one_ + H)
                    v_tokens(one_)

                def filler(i):
                    if two is not None and i == 0:
                        expert_weights(two, n + 1)
                        expert_gate(two, n + 1)
                    elif two is not None and i == 1:
                        expert_up(two, n + 1)
                    elif two is not None:
                        expert_down(two, n)
                for n in range(NCH):
                    if one_ is not None:
                        scan(one_, n, filler)
                    else:
                        for i in range(3):
                            filler(i)
                if two is not None:
                    expert_down(two, PAIRS)
                if one_ is not None:
                    delta_tokens(one_)
                if two is not None:
                    expert_tokens(two)

            tile(0, None)
            eng.wait_ge(w_late, W_LATE)
            eng.wait_ge(wprep, 6)
            with eng.Fori(1, TILES) as k:
                tile(k, k - 1)
            tile(None, TILES - 1)


LOOP_STEPS = 119

_INS = ["hidden_states", "w_q", "w_k", "w_v", "w_b", "conv_q_w", "conv_k_w", "conv_v_w", "fir1", "fir3", "fir7",
        "fir15", "fir31", "gate_w1", "gate_b1", "gate_w2", "gate_b2", "norm_w", "w_o"]
_FFN = ["Wg", "W1", "W2", "Ws1", "Ws2"]


def kernel(**inputs):
    import numpy as _np
    import concourse.bacc as _bacc
    from concourse import mybir as _mybir
    from concourse.bass_utils import run_bass_kernel_spmd as _run

    nc = _bacc.Bacc("TRN2", target_bir_lowering=False, num_devices=1)
    arrays, args = {}, []
    for name in ["L0_attn_" + n for n in _INS] + ["L0_ffn_" + n for n in _FFN]:
        arrays[name] = _np.ascontiguousarray(inputs[name])
    arrays["shape_constants"] = shape_constants()
    for name, a in arrays.items():
        args.append(nc.dram_tensor(name, a.shape, _mybir.dt.from_np(a.dtype), kind="ExternalInput").ap())
    out = nc.dram_tensor("out", (NB, SEQ, D), _mybir.dt.float32, kind="ExternalOutput").ap()
    build(nc, *args, out)
    r = _run(nc, [arrays], core_ids=[0])
    return r.results[0]["out"]
```

```python
import concourse.bass as bass
from concourse import mybir
from contextlib import ExitStack
import numpy as np

NB, SEQ, D = 2, 1024, 128
H, DH, C = 4, 32, 32
TILES = 4
TB = SEQ // TILES
TT = NB * TB
NCH = TB // C
G = NB * NCH
A = 4
Q = TB // A
FIRS = (31, 15, 7, 3)
MS = [(k + 3 + 3) // 4 for k in FIRS]
MX = MS[0]
NS = 7
STREAM = (4, 3, 2, 1, 0, 5, 6)
E, HE, HS = 16, 64, 128
PAIRS = E // 2
LN_EPS, L2_EPS, RMS_EPS, GATE_EPS = 1e-5, 1e-6, 1e-5, 0.02
LEVELS = 5

C_ID = 0
C_ONES = 128
C_I32 = 256
C_LOW = 288
C_UP = 320
C_LEV = 352
C_HEAD = 512
C_SEL = 512 + 1024
C_END = C_SEL + PAIRS * 128


def shape_constants():
    c = np.zeros((128, C_END), np.float32)
    p, j, r = np.arange(128)[:, None], np.arange(32)[None, :], np.arange(128)[None, :]
    i = p % 32
    c[:, C_ID:C_ID + 128] = p == r
    c[:, C_ONES:C_ONES + 128] = p // 32 == r // 32
    c[:, C_I32:C_I32 + 32] = i == j
    c[:, C_LOW:C_LOW + 32] = j < i
    c[:, C_UP:C_UP + 32] = i <= j
    for l in range(LEVELS):
        s = 1 << l
        c[:, C_LEV + 32 * l:C_LEV + 32 * l + 32] = (i // (2 * s) == j // (2 * s)) & (i // s % 2 == 1) & (j // s % 2 == 0)
    for t in range(2 * A):
        c[:32, C_HEAD + 128 * t:C_HEAD + 128 * t + 128] = p[:32] == H * t + r // DH
    for t in range(PAIRS):
        c[:48, C_SEL + 128 * t:C_SEL + 128 * t + 128] = (p[:48] % 16) == 2 * t + r // 64
    return c


def build(nc, x_dram, w_q, w_k, w_v, w_b, conv_q, conv_k, conv_v, fir1, fir3, fir7, fir15, fir31,
          gate_w1, gate_b1, gate_w2, gate_b2, norm_w, w_o, Wg, W1, W2, Ws1, Ws2, consts, out):
    f32, bf16 = mybir.dt.float32, mybir.dt.bfloat16
    ALU, ACT, AX = mybir.AluOpType, mybir.ActivationFunctionType, mybir.AxisListType

    ctx = ExitStack()
    with ctx:
        def sb(name, shape, dt=f32):
            return ctx.enter_context(nc.sbuf_tensor(name, shape, dt))

        def sem(name):
            return ctx.enter_context(nc.semaphore(name))

        cst = sb("cst", [128, C_HEAD])
        ident = cst[:, C_ID:C_ID + 128]
        eye32 = cst[:, C_I32:C_I32 + 32]
        low = cst[:, C_LOW:C_LOW + 32]
        up = cst[:, C_UP:C_UP + 32]
        headsel = sb("headsel", [32, 2 * A, 128])
        selb = sb("selb", [48, PAIRS, 128], bf16)
        identb = sb("identb", [128, 128], bf16)
        ffn = sb("ffn", [128, 6, TT])
        sg, sc, hT = ffn[:, 0:2, :], ffn[:, 2:4, :], ffn[:, 4:6, :]
        diag = ffn[:, 0:3, :].rearrange("p i (t n) -> p i t n", t=4)
        wraw = ffn[:, 3, 0:384].rearrange("p (i n) -> p i n", i=3)
        wrawT = ffn[:, 4, 0:384].rearrange("p (i n) -> p i n", i=3)
        convw = sb("convw", [128, 3, 4])
        wtap = sb("wtap", [128, 3, 4, 128])
        wb_raw = sb("wb_raw", [128, H])
        wb_rep = sb("wb_rep", [128, H, 32])
        firw = [sb(f"firw{s}", [128, H, 4 * MS[s]]) for s in range(4)]
        toep = [sb(f"toep{m}", [128, H, sum(m < x for x in MS), A, 32]) for m in range(MX)]
        fir1_row = sb("fir1_row", [128, 128])
        g1x = sb("g1x", [128, 2 * D])
        g1s = sb("g1s", [NS * H, 2 * D])
        gb1 = sb("gb1", [128, 2])
        g2raw = sb("g2raw", [128, 2, NS * H])
        g2 = sb("g2", [128, 2, NS, H])
        gb2raw = sb("gb2raw", [128, NS * H])
        gb2 = sb("gb2", [128, NS, H])
        normw = sb("normw", [128, 1])
        wo_raw = sb("wo_raw", [128, 128])
        sel = sb("sel", [48, PAIRS * 128])
        wo = sb("wo", [128, 128])
        wg_raw = sb("wg_raw", [E, 128])
        wgT = sb("wgT", [128, E])
        w1 = sb("w1", [128, PAIRS, 2, 2, HE])
        w2 = sb("w2", [128, PAIRS, 128])
        ws1 = sb("ws1", [128, 2 * HS])
        ws2 = sb("ws2", [128, 128])
        one = sb("one", [128, 1])

        x_all = sb("x_all", [128, TILES + 1, A, 128])
        st = sb("st", [128, A, 6])
        mv = sb("mv", [128, A, 2])
        rs = sb("rs", [128, 4, 2 * A * H])
        rnT = sb("rnT", [2 * A * H, 128])
        spare = sb("spare", [1, 1])
        aspare = sb("aspare", [128, 1])
        pmix = sb("pmix", [128, 4, A, H, DH])
        xn = sb("xn", [128, A, 128])
        xnT = sb("xnT", [128, NB, 3 + TB])
        kqs = sb("kqs", [128, 2, TT])
        vF = sb("vF", [128, TT])
        vP = sb("vP", [128, TT])
        sq = sb("sq", [128, 2, TT])
        kq = sb("kq", [128, G, 2, C])
        beta = sb("beta", [128, TT])
        betaB = sb("betaB", [128, G, C])
        v4 = sb("v4", [128, H, 8 + Q, NB])
        vB = sb("vB", [128, G, C])
        Lc = sb("Lc", [128, G, C])
        LT = sb("LT", [128, G, C])
        X = sb("X", [128, G, C])
        XT = sb("XT", [128, G, C])
        M1 = sb("M1", [128, G, C])
        tmpB = M1
        kB = sb("kB", [128, G, C])
        attnT = sb("attnT", [128, G, C])
        S = sb("S", [128, 2, NB, DH])
        r = sb("r", [128, NB, DH])
        u = sb("u", [128, NB, DH])
        oB = Lc
        oF = vP
        SM = sb("SM", [128, NS, A, H, DH])
        stat = sb("stat", [128, A, NS, H])
        statT = ffn[0:NS * H, 2, :]
        hid = ffn[:, 0:2, :]
        z = sb("z", [128, A, NS * H])
        za = sb("za", [128, A, NS * H])
        ze = sb("ze", [128, A, NS * H])
        zl = sb("zl", [128, A, NS * H])
        wt = sb("wt", [128, A, NS, H])
        wsum = sb("wsum", [128, A, H])
        prod = hid.rearrange("p i (a h c) -> p i a h c", a=A, h=H)
        acc = ffn[:, 4:6, :].rearrange("p i (a h c) -> p i a h c", a=A, h=H)
        ss = sb("ss", [128, A, H])
        oT = sb("oT", [128, TT])
        y1 = sb("y1", [128, A, 128])
        x1 = sb("x1", [128, A, 128])
        x2n = y1
        x2T = sb("x2T", [128, TT])
        rl = sb("rl", [128, A, E])
        top8 = sb("top8", [128, A, 8])
        want2 = sb("want2", [128, A, 8])
        rrep = sb("rrep", [128, A, E])
        re = sb("re", [128, A, E])
        rsum = sb("rsum", [128, A])
        cw = sb("cw", [128, A, E])
        cwr = sb("cwr", [128, 2, A, E])
        cw3 = sb("cw3", [128, A, 8, E], bf16)
        cwT = sb("cwT", [48, TT], bf16)
        zT = oT

        PS = ctx.enter_context(nc.psum_tensor("PS", [128, 8 * 512], f32))

        FIR_BANKS = (7, 3, 5, 4)
        DVE_STREAMS = 4
        LEVEL_STEPS = 4 * (LEVELS - 1)

        def bank(i, n=1):
            return PS[:, 512 * i:512 * (i + n)]

        w_in = sem("w_in")
        w_late = sem("w_late")
        x0_in = sem("x0_in")
        x_in = sem("x_in")
        init = sem("init")
        wprep_pe = sem("wprep_pe")
        wprep = sem("wprep")
        toep_ready = sem("toep_ready")
        dve = sem("dve")
        taps_in = sem("taps_in")
        signals = """
            xn_ready     x normalised (DVE)
            xnT_ps       ... transposed, in PSUM
            halo         the last 3 tokens of the tile before are in front of xnT
            xnT_ready    x feature-major in SBUF
            v_ps         v projected and convolved, in PSUM
            kq_ps        k, then q: the same
            beta_ps      beta's logits, in PSUM
            kq_silu      silu of k, then of q
            sq_done      their squares
            silu_done    v feature-major
            vP_done      v in the column order of the token-major streams
            beta_exp     tanh(beta's logits / 2)
            v4_halo      the last 8 quads of the tile before are in front of v4
            v4_ready     v4 of heads 0 and 1, then of 2 and 3
            ssq_ps       sums of squares per head and token
            rn_ready     inverse norms (DVE)
            rnT_ps       ... transposed, in PSUM
            rnT_ready    ... in SBUF
            rnF_ps       ... a row for each feature, in PSUM
            kq_ready     k and q normalised, k transposed
            gram_ps      k.k and k.q of the chunks
            x_ready      a half of the inverse so far: 2 at the start, then 2 a level
            m1_ps        L X of half the groups
            m1_ready     ... masked, in SBUF
            m2_ps        X (L X) of half the groups
            T_ready      a half of (T diag(beta))^T
            ks_ps        K S of a chunk
            r_ready      v - K S
            u_ps         u = T diag(beta) r, in PSUM
            u_ready      ... in SBUF
            ds_ps        K^T u
            s_ready      the state after a chunk (1 for the zero state)
            o_ps         all outputs of a tile's scan
            oF_ready     ... feature-major in SBUF
            fir_ps       a head's four FIRs, in PSUM
            fir_out      ... in the streams' buffer
            vt_ps        v token-major, in PSUM
            vt_out       ... in the streams' buffer
            dt_ps        the scan's result token-major, in PSUM
            dt_out       ... in the streams' buffer
            mix_in       the one-tap stream (Pool)
            stat_ready   the streams' mean absolute values
            statT_ps     ... transposed, in PSUM
            statT_ready  ... in SBUF
            hidx_ps      the gate's first layer, x's part
            hid_ps       a half of the gate's first layer
            hid_ready    ... after gelu
            logit_ps     the gate's logits, in PSUM
            z_ready      ... with the bias
            zabs         |z|
            z_exp        exp(-|z|)
            z_ln         ln(1 + exp(-|z|))
            wt_ready     the streams' weights
            pool_mix     Pool's five steps of the mix
            mixed        the streams mixed and normalised
            oT_ps        ... transposed, in PSUM
            oT_ready     ... in SBUF
            y_ps         the attention's output
            x2_ready     the experts' input
            x2T_ps       ... transposed, in PSUM
            x2T_ready    ... in SBUF
            router_ps    the router's logits
            re_in        ... less their maximum
            re_out       ... exponentials
            cw_ready     the experts' weights, in three parts
            cwT_ps       ... transposed, in PSUM
            cwT_ready    ... in SBUF
            gate_ps      an expert's gate
            wts_ps       a pair's weights, a row for each hidden unit
            up_ps        an expert's up projection
            sg_ready     silu of the gate
            sc_ready     ... times the weight
            h_ready      an expert's hidden layer
            z_ps         an expert's part of the sum
            zT_ready     the sum in SBUF
            yo_ps        ... token-major, in PSUM
            y_ready      the tile's result
            y_stored     ... in DRAM
        """
        s = {line.split()[0]: sem(line.split()[0]) for line in signals.strip().splitlines()}

        block = ctx.enter_context(nc.Block())

        x_v = x_dram.rearrange("b (t q a) d -> b q t (a d)", t=TILES, a=A)
        o_v = out.rearrange("b (t q a) d -> b q t (a d)", t=TILES, a=A)

        early = [
            (cst[:, :], consts[:, 0:C_HEAD]),
            (convw[:, 0, :], conv_q), (convw[:, 1, :], conv_k), (convw[:, 2, :], conv_v),
            (wb_raw[:, :], w_b), (wg_raw[:, :], Wg),
            (headsel[:, :, :], consts[0:32, C_HEAD:C_SEL].rearrange("p (t n) -> p t n", n=128)),
        ]
        late = [
            (fir1_row[:, :], fir1.rearrange("c k -> (c k)").partition_broadcast(128)),
            (g1x[:, :], gate_w1[0:D, :]),
            (gb1[:, :], gate_b1.rearrange("(a p) -> p a", p=128)),
            (g2raw[:, :, :], gate_w2.rearrange("(a p) n -> p a n", p=128)),
            (gb2raw[:, :], gate_b2.partition_broadcast(128)),
            (wo_raw[:, :], w_o), (sel[:, :], consts[0:48, C_SEL:C_END]),
            (w2[:, :, :], W2.rearrange("(t e) h d -> (e h) t d", e=2)),
            (ws1[:, :], Ws1), (ws2[:, :], Ws2),
        ]
        late += [(g1s[4 * i:4 * i + 4, :], gate_w1[D + 4 * STREAM[i]:D + 4 * STREAM[i] + 4, :]) for i in range(NS)]
        late += [(normw[32 * h:32 * h + 32, :], norm_w.rearrange("(c a) -> c a", a=1)) for h in range(H)]
        late += [(w1[:, :, i, e, :], W1.rearrange("(t e) d (i h) -> i e d t h", e=2, i=2)[i, e]) for i in range(2) for e in range(2)]
        W_IN, W_LATE = 16 * (len(early) + 3), 16 * len(late)

        POOL_TOEP = 2

        def toeplitz(eng, m, i, a):
            zp = 4 * MS[i] - 1 - 4 * m - a
            return eng.tensor_tensor(out=toep[m][:, :, i, a, :], in0=eye32.unsqueeze(1).to_broadcast([128, H, 32]),
                                     in1=firw[i][:, :, zp:zp + 1].to_broadcast([128, H, 32]), op=ALU.mult)

        @block.gpsimd
        def _(eng):
            eng.memset(S[:, :, :, :], 0.0).then_inc(s["s_ready"], 1)
            eng.memset(xnT[:, :, :], 0.0).then_inc(init, 1)
            eng.memset(v4[:, :, :, :], 0.0).then_inc(init, 1)
            eng.memset(one[:, :], 1.0).then_inc(init, 1)
            eng.memset(cw3[:, :, :, :], 0.0).then_inc(init, 1)
            eng.memset(x_all[:, TILES, :, :], 0.0).then_inc(init, 1)
            for i in range(4):
                eng.memset(firw[i][:, :, :], 0.0).then_inc(init, 1)
            eng.wait_ge(init, 9)
            with nc.allow_non_contiguous_dma("short rows of taps"):
                for i, w in enumerate((fir31, fir15, fir7, fir3)):
                    for b in range(4):
                        eng.dma_start(firw[i][32 * b:32 * b + 32, :, 5 - b:5 - b + FIRS[i]],
                                      w.rearrange("(h c) k -> c h k", h=H)).then_inc(taps_in, 16)
            eng.wait_ge(taps_in, 256)
            eng.wait_ge(w_in, W_IN)
            for m in range(POOL_TOEP):
                for i in range(4):
                    if m < MS[i]:
                        for a in range(A):
                            t = toeplitz(eng, m, i, a)
            t.then_inc(toep_ready, 1)
            eng.wait_ge(w_late, W_LATE)

            def fir1_stream(k):
                eng.wait_ge(s["vt_out"], k + 1)
                eng.tensor_tensor(out=SM[:, 4, :, :, :], in0=SM[:, 6, :, :, :],
                                  in1=fir1_row[:, :].rearrange("p (h c) -> p h c", h=H).unsqueeze(1)
                                  .to_broadcast([128, A, H, DH]), op=ALU.mult).then_inc(s["mix_in"], 1)

            def mix(k):
                eng.wait_ge(s["wt_ready"], k + 1)
                for i in range(3):
                    eng.tensor_tensor(out=pmix[:, i, :, :, :], in0=SM[:, DVE_STREAMS + i, :, :, :],
                                      in1=wt[:, :, DVE_STREAMS + i, :].unsqueeze(3).to_broadcast([128, A, H, DH]),
                                      op=ALU.mult).then_inc(s["pool_mix"], 1)
                eng.wait_ge(s["pool_mix"], 5 * k + 2)
                eng.tensor_tensor(out=pmix[:, 3, :, :, :], in0=pmix[:, 0, :, :, :], in1=pmix[:, 1, :, :, :],
                                  op=ALU.add).then_inc(s["pool_mix"], 1)
                eng.wait_ge(s["pool_mix"], 5 * k + 4)
                eng.tensor_tensor(out=pmix[:, 0, :, :, :], in0=pmix[:, 3, :, :, :], in1=pmix[:, 2, :, :, :],
                                  op=ALU.add).then_inc(s["pool_mix"], 1)

            fir1_stream(0)
            with eng.Fori(1, TILES) as k:
                mix(k - 1)
                fir1_stream(k)
            mix(TILES - 1)

        @block.sync
        def _(eng):
            with nc.allow_non_contiguous_dma("weights, once"):
                for dst, src in early:
                    eng.dma_start(dst, src).then_inc(w_in, 16)
                for dst, src in late:
                    eng.dma_start(dst, src).then_inc(w_late, 16)
            with eng.Fori(0, TILES) as k:
                eng.wait_ge(s["y_ready"], k + 1)
                for b in range(NB):
                    eng.dma_start(o_v[b, :, bass.ds(k, 1), :], x_all[b:128:2, bass.ds(k, 1), :, :].rearrange("p k a d -> p (k a) d")).then_inc(s["y_stored"], 16)
            eng.wait_ge(s["y_stored"], 32 * TILES)

        @block.scalar
        def _(eng):
            for t in range(TILES):
                for b in range(NB):
                    eng.dma_start(x_all[b:128:2, t, :, :],
                                  x_v[b, :, t, :]).then_inc(x_in if t else x0_in, 16)
                if t == 0:
                    for i, w in enumerate((w_q, w_k, w_v)):
                        eng.dma_start(wraw[:, i, :], w).then_inc(w_in, 16)
            eng.wait_ge(init, 9)

            def tokens_to_features(k):
                if not isinstance(k, int):
                    eng.wait_ge(s["beta_ps"], k)
                    eng.wait_ge(s["hidx_ps"], k)
                eng.activation(xnT[:, :, 0:3], xnT[:, :, TB:TB + 3], ACT.Copy).then_inc(s["halo"], 1)
                eng.wait_ge(s["xnT_ps"], k + 1)
                eng.wait_ge(s["halo"], k + 1)
                eng.activation(xnT[:, :, 3:3 + TB].rearrange("p b (q a) -> p a q b", a=A),
                               bank(0).rearrange("p (a q b) -> p a q b", a=A, b=NB), ACT.Copy).then_inc(s["xnT_ready"], 1)

            def values(k):
                eng.wait_ge(s["v_ps"], k + 1)
                eng.activation(vF[:, :], bank(3), ACT.Silu).then_inc(s["silu_done"], 1)
                eng.activation(vP[:, :].rearrange("p (a q b) -> p b q a", a=A, b=NB),
                               bank(3).rearrange("p (b q a) -> p b q a", a=A, b=NB), ACT.Silu).then_inc(s["vP_done"], 1)

            def silus(k):
                for i in range(2):
                    phases(k, i)
                    eng.wait_ge(s["kq_ps"], 2 * k + i + 1)
                    eng.activation(kqs[:, i, :], bank(1 + i), ACT.Silu).then_inc(s["kq_silu"], 1)
                    eng.wait_ge(s["kq_silu"], 2 * k + i + 1)
                    eng.activation(sq[:, i, :], kqs[:, i, :], ACT.Square).then_inc(s["sq_done"], 1)
                    if i == 0:
                        eng.wait_ge(s["beta_ps"], k + 1)
                        eng.activation(beta[:, :], bank(0), ACT.Tanh, scale=0.5).then_inc(s["beta_exp"], 1)

            def phases(k, half):
                if half == 0:
                    eng.activation(v4[:, :, 0:8, :], v4[:, :, Q:Q + 8, :], ACT.Copy).then_inc(s["v4_halo"], 1)
                    eng.wait_ge(s["silu_done"], k + 1)
                    eng.wait_ge(s["v4_halo"], k + 1)
                for h in range(2 * half, 2 * half + 2):
                    for b in range(4):
                        t = eng.activation(v4[32 * b:32 * b + 32, h, 8:8 + Q, :],
                                           vF[32 * h:32 * h + 32, :].rearrange("p (n q a) -> p q n a", n=NB, a=4)[:, :, :, b],
                                           ACT.Copy)
                t.then_inc(s["v4_ready"], 1)

            def norms_back(k):
                eng.wait_ge(s["rnT_ps"], k + 1)
                eng.activation(rnT[:, :], bank(1)[0:2 * A * H, 128:256], ACT.Copy).then_inc(s["rnT_ready"], 1)

            def scan_u(k, n):
                eng.wait_ge(s["u_ps"], NCH * k + n + 1)
                eng.activation(u[:, :, :], bank(0)[:, 64:128].rearrange("p (b i) -> p b i", b=NB), ACT.Copy).then_inc(s["u_ready"], 1)

            def fir_out(k, h):
                if h == 0 and not isinstance(k, int):
                    eng.wait_ge(s["mixed"], k)
                eng.wait_ge(s["fir_ps"], 4 * k + h + 1)
                eng.activation(SM[:, 0:4, :, h, :],
                               bank(FIR_BANKS[h]).rearrange("p (s a c) -> p s a c", s=4, a=A),
                               ACT.Copy).then_inc(s["fir_out"], 1)

            def v_stream(k):
                eng.wait_ge(s["vt_ps"], k + 1)
                eng.activation(SM[:, 6, :, :, :].rearrange("p a h c -> p (a h c)"), bank(2), ACT.Copy).then_inc(s["vt_out"], 1)

            def delta_stream(k):
                eng.wait_ge(s["dt_ps"], k + 1)
                eng.activation(SM[:, 5, :, :, :].rearrange("p a h c -> p (a h c)"), bank(3), ACT.Copy).then_inc(s["dt_out"], 1)

            def gate_statistics(k):
                eng.wait_ge(s["statT_ps"], k + 1)
                eng.activation(statT.rearrange("s (b q a) -> s a q b", b=NB, a=A),
                               bank(7)[0:NS * H, :].rearrange("s (a q b) -> s a q b", a=A, b=NB),
                               ACT.Copy, scale=1.0 / DH).then_inc(s["statT_ready"], 1)

            def gate(k):
                for i in range(2):
                    eng.wait_ge(s["hid_ps"], 2 * k + i + 1)
                    eng.activation(hid[:, i, :].rearrange("p (a q b) -> p b q a", a=A, b=NB),
                                   bank(4 + i).rearrange("p (b q a) -> p b q a", a=A, b=NB), ACT.Gelu, bias=gb1[:, i:i + 1]).then_inc(s["hid_ready"], 1)

            def softplus(k):
                eng.activation(aspare[:, :], one[:, :], ACT.Exp)
                eng.wait_ge(s["z_ready"], k + 1)
                eng.activation(za[:, :, :], z[:, :, :], ACT.Abs).then_inc(s["zabs"], 1)
                eng.wait_ge(s["zabs"], k + 1)
                eng.activation(ze[:, :, :], za[:, :, :], ACT.Exp, scale=-1.0).then_inc(s["z_exp"], 1)
                eng.wait_ge(s["z_exp"], k + 1)
                eng.activation(zl[:, :, :], ze[:, :, :], ACT.Ln, bias=one[:, :]).then_inc(s["z_ln"], 1)

            def o_features(k):
                eng.wait_ge(s["oT_ps"], k + 1)
                eng.activation(oT[:, :], bank(6), ACT.Copy).then_inc(s["oT_ready"], 1)

            def x2_features(k):
                eng.wait_ge(s["x2T_ps"], k + 1)
                eng.activation(x2T[:, :], bank(6), ACT.Copy).then_inc(s["x2T_ready"], 1)

            def router_exp(k):
                eng.wait_ge(s["re_in"], k + 1)
                eng.activation(re[:, :, :], rrep[:, :, :], ACT.Exp).then_inc(s["re_out"], 1)

            def expert(k, j):
                n = (PAIRS + 1) * k + j
                eng.wait_ge(s["gate_ps"], n + 1)
                if j >= 2:
                    eng.wait_ge(s["h_ready"], n - 1)
                eng.activation(sg[:, j % 2, :], bank(5), ACT.Silu).then_inc(s["sg_ready"], 1)

            def z_features(k):
                eng.wait_ge(s["z_ps"], (PAIRS + 1) * (k + 1))
                eng.activation(zT[:, :], bank(7), ACT.Copy).then_inc(s["zT_ready"], 1)

            def tile(one_, two):
                if one_ is not None:
                    tokens_to_features(one_)
                if two is not None:
                    gate_statistics(two)
                    gate(two)
                    softplus(two)
                if one_ is not None:
                    values(one_)
                    silus(one_)
                    norms_back(one_)
                if two is not None:
                    o_features(two)
                if one_ is not None:
                    for h in range(3):
                        fir_out(one_, h)
                if two is not None:
                    x2_features(two)
                if one_ is not None:
                    fir_out(one_, 3)
                if two is not None:
                    router_exp(two)
                    expert(two, 0)
                if one_ is not None:
                    v_stream(one_)
                for n in range(NCH):
                    if one_ is not None:
                        scan_u(one_, n)
                    if two is not None:
                        expert(two, n + 1)
                if two is not None:
                    z_features(two)
                if one_ is not None:
                    delta_stream(one_)

            tile(0, None)
            eng.wait_ge(w_late, W_LATE)
            with eng.Fori(1, TILES) as k:
                tile(k, k - 1)
            tile(None, TILES - 1)

        @block.vector
        def _(eng):
            cnt = [0]
            base = [0]

            def carry_wait():
                V.memset(spare[0:1, 0:1], 0.0)

            def link(ins):
                cnt[0] += 1
                ins.then_inc(dve, 1)
                eng.wait_ge(dve, base[0] + cnt[0])

            V = nc.vector

            def bc(ap, n=G):
                return ap.unsqueeze(1).to_broadcast([128, n, 32])

            def inv_sqrt(n):
                v, y, t = rs[:, 0, 0:n], rs[:, 1, 0:n], rs[:, 2, 0:n]
                i32 = mybir.dt.int32
                link(V.tensor_scalar(y.bitcast(i32), v.bitcast(i32), 1, None, ALU.logical_shift_right))
                link(V.tensor_scalar(y.bitcast(i32), y.bitcast(i32), -1.0, float(0x5F3759DF), ALU.mult, ALU.add))
                for _ in range(3):
                    link(V.tensor_tensor(t, y, y, ALU.mult))
                    link(V.scalar_tensor_tensor(out=t, in0=t, scalar=-0.5, in1=v, op0=ALU.mult, op1=ALU.mult))
                    link(V.scalar_tensor_tensor(out=y, in0=t, scalar=1.5, in1=y, op0=ALU.add, op1=ALU.mult))

            def moments(src):
                for a in range(A):
                    t = V.bn_stats(st[:, a, :], src(a))
                link(t)
                carry_wait()
                for a in range(A):
                    t = V.bn_aggr(mv[:, a, :], st[:, a, :])
                link(t)
                link(V.tensor_scalar(rs[:, 0, 0:A], mv[:, :, 1], LN_EPS, None, ALU.add))

            def scaled(src, dst):
                for a in range(A):
                    t = V.tensor_scalar(dst[:, a, :], src(a), mv[:, a, 0:1], rs[:, 1, a:a + 1],
                                        ALU.subtract, ALU.mult)
                return t

            def layer_norm(src, dst):
                moments(src)
                inv_sqrt(A)
                return scaled(src, dst)

            def norm_x(k, step):
                x = lambda a: x_all[:, bass.ds(k, 1), a, :].rearrange("p k d -> p (k d)")
                if step == 0:
                    moments(x)
                elif step == 1:
                    inv_sqrt(A)
                else:
                    scaled(x, xn).then_inc(s["xn_ready"], 1)

            eng.wait_ge(x0_in, 32)
            for step in range(3):
                norm_x(0, step)
            eng.wait_ge(w_in, W_IN)
            eng.wait_ge(init, 9)
            V.tensor_copy(identb[:, :], ident)
            V.tensor_copy(wb_rep[:, :, :], wb_raw[:, :].unsqueeze(2).to_broadcast([128, H, 32]))
            for i in range(3):
                for t in range(4):
                    last = V.tensor_scalar(diag[:, i, t, :], ident, convw[:, i, t:t + 1], None, ALU.mult)
            last.then_inc(wprep, 1)
            eng.wait_ge(wprep_pe, 1)
            V.tensor_copy(wrawT[:, :, :], bank(0)[:, 0:384].rearrange("p (i n) -> p i n", i=3))
            V.tensor_copy(wgT[:, :], bank(0)[:, 384:400]).then_inc(wprep, 1)
            for i in range(3):
                eng.wait_ge(wprep_pe, 2 + i)
                V.tensor_copy(wtap[:, i, :, :], bank(1 + i).rearrange("p (t n) -> p t n", t=4)).then_inc(wprep, 1)

            def late_weights():
                eng.wait_ge(w_late, W_LATE)
                V.tensor_copy(selb[:, :, :], sel[:, :].rearrange("e (t p) -> e t p", t=PAIRS))
                V.tensor_scalar(wo[:, :], wo_raw[:, :], normw[:, 0:1], None, ALU.mult)
                for i in range(NS):
                    V.tensor_copy(gb2[:, i, :], gb2raw[:, STREAM[i]::NS])
                for i in range(NS):
                    t = V.tensor_copy(g2[:, :, i, :], g2raw[:, :, STREAM[i]::NS])
                t.then_inc(wprep, 1)

            def feature_groups(ap):
                return ap.rearrange("p (g i) -> p g i", g=G)

            def values_and_beta(k):
                eng.wait_ge(s["silu_done"], k + 1)
                V.transpose(vB[:, :, :], feature_groups(vF[:, :]))
                eng.wait_ge(s["beta_exp"], k + 1)
                link(V.tensor_scalar(beta[:, :], beta[:, :], 0.5, 0.5, ALU.mult, ALU.add))
                V.transpose(betaB[:, :, :], feature_groups(beta[:, :]))

            def inverse_norms(k):
                eng.wait_ge(s["ssq_ps"], k + 1)
                link(V.tensor_scalar(rs[:, 0, :], bank(1)[:, 0:2 * A * H], L2_EPS, None, ALU.add))
                inv_sqrt(2 * A * H)
                V.tensor_copy(rs[:, 3, :], rs[:, 1, :]).then_inc(s["rn_ready"], 1)

            def normalise(k):
                eng.wait_ge(s["rnF_ps"], k + 1)
                for i in range(2):
                    t = V.tensor_tensor(kq[:, :, i, :], feature_groups(kqs[:, i, :]), feature_groups(bank(1 + i)), ALU.mult)
                link(t)
                V.transpose(kB[:, :, :], kq[:, :, 0, :]).then_inc(s["kq_ready"], 1)

            def gram_out(k):
                eng.wait_ge(s["gram_ps"], k + 1)
                for f in range(2):
                    gram = bank(1 + f).rearrange("p (g w i) -> p g w i", g=G // 2, w=2)
                    gs = slice(8 * f, 8 * f + 8)
                    V.tensor_tensor(attnT[:, gs, :], gram[:, :, 1, :], bc(up, 8), ALU.mult)
                    t = V.tensor_tensor(tmpB[:, gs, :], gram[:, :, 0, :], bc(low, 8), ALU.mult)
                link(t)
                link(V.tensor_tensor(Lc[:, :, :], tmpB[:, :, :], betaB[:, :, :], ALU.mult))
                link(V.transpose(LT[:, :, :], Lc[:, :, :]))
                link(V.tensor_tensor(M1[:, :, :], Lc[:, :, :], bc(cst[:, C_LEV:C_LEV + 32]), ALU.mult))
                V.tensor_tensor(X[:, :, :], bc(eye32), M1[:, :, :], ALU.subtract).then_inc(s["x_ready"], 2)
                eng.wait_ge(s["x_ready"], 10 * k + 2)
                V.transpose(XT[:, :, :], X[:, :, :])

            def level(k, i):
                l, f = 1 + i // 4, i % 2
                gs = slice(8 * f, 8 * f + 8)
                n = 8 * k + 2 * (l - 1) + f + 1
                if i % 4 < 2:
                    lev = cst[:, C_LEV + 32 * l:C_LEV + 32 * l + 32]
                    eng.wait_ge(s["m1_ps"], n)
                    V.tensor_tensor(M1[:, gs, :], bank(1 + f)[:, 0:256].rearrange("p (g i) -> p g i", g=8),
                                    bc(lev, 8), ALU.mult).then_inc(s["m1_ready"], 1)
                else:
                    eng.wait_ge(s["m2_ps"], n)
                    V.tensor_tensor(X[:, gs, :], X[:, gs, :], bank(1 + f)[:, 256:512].rearrange("p (g i) -> p g i", g=8),
                                    ALU.subtract).then_inc(s["x_ready"], 1)
                    eng.wait_ge(s["x_ready"], 10 * k + 2 * l + f + 1)
                    if l < LEVELS - 1:
                        V.transpose(XT[:, gs, :], X[:, gs, :])
                    else:
                        link(V.transpose(XT[:, gs, :], X[:, gs, :]))
                        V.tensor_tensor(XT[:, gs, :], XT[:, gs, :], betaB[:, gs, :], ALU.mult).then_inc(s["T_ready"], 1)

            def scan_r(k, n):
                eng.wait_ge(s["ks_ps"], NCH * k + n + 1)
                V.tensor_tensor(r[:, :, :], vB[:, :, :].rearrange("p (b n) i -> p b n i", b=NB)[:, :, n, :],
                                bank(0)[:, 0:64].rearrange("p (b i) -> p b i", b=NB), ALU.subtract).then_inc(s["r_ready"], 1)

            def scan_s(k, n):
                eng.wait_ge(s["ds_ps"], NCH * k + n + 1)
                V.tensor_tensor(S[:, (n + 1) % 2, :, :], S[:, n % 2, :, :],
                                bank(0)[:, 128:192].rearrange("p (b i) -> p b i", b=NB), ALU.add).then_inc(s["s_ready"], 1)

            def stats(i):
                return V.tensor_reduce(out=stat[:, :, i, :], in_=SM[:, i, :, :, :], op=ALU.add, axis=AX.X,
                                       apply_absolute_value=True)

            def delta_out(k):
                eng.wait_ge(s["o_ps"], k + 1)
                link(V.tensor_copy(oB[:, :, :], feature_groups(bank(3))))
                eng.wait_ge(s["vt_ps"], k + 1)
                V.transpose(oF[:, :].rearrange("p (a q b) -> p b q a", a=A, b=NB),
                            oB[:, :, :].rearrange("p g i -> p (g i)").rearrange("p (b q a) -> p b q a", b=NB, a=A)).then_inc(s["oF_ready"], 1)

            def statistics(k, n):
                if n == 0:
                    eng.wait_ge(s["fir_out"], H * (k + 1))
                if n < 4:
                    stats(n)
                elif n == 4:
                    eng.wait_ge(s["vt_out"], k + 1)
                    stats(6)
                elif n == 5:
                    eng.wait_ge(s["mix_in"], k + 1)
                    stats(4)

            def delta_statistics(k):
                eng.wait_ge(s["dt_out"], k + 1)
                stats(5).then_inc(s["stat_ready"], 1)

            def logits_out(k):
                eng.wait_ge(s["logit_ps"], k + 1)
                V.tensor_tensor(z[:, :, :], bank(7)[:, 0:A * NS * H].rearrange("p (a n) -> p a n", a=A),
                                gb2[:, :, :].rearrange("p s h -> p (s h)").unsqueeze(1).to_broadcast([128, A, NS * H]), ALU.add).then_inc(s["z_ready"], 1)

            def mix_weights(k):
                eng.wait_ge(s["z_ln"], k + 1)
                link(V.scalar_tensor_tensor(out=z[:, :, :], in0=z[:, :, :], scalar=0.0, in1=zl[:, :, :], op0=ALU.max, op1=ALU.add))
                zf = z[:, :, :].rearrange("p a (s h) -> p a s h", s=NS)
                link(V.tensor_scalar(z[:, :, :], z[:, :, :], GATE_EPS, None, ALU.add))
                link(V.tensor_reduce(out=wsum[:, :, :], in_=z[:, :, :].rearrange("p a (s h) -> p a h s", s=NS), op=ALU.add, axis=AX.X))
                link(V.reciprocal(wsum[:, :, :], wsum[:, :, :]))
                V.tensor_tensor(wt[:, :, :, :], zf, wsum[:, :, :].unsqueeze(2).to_broadcast([128, A, NS, H]), ALU.mult).then_inc(s["wt_ready"], 1)
                eng.wait_ge(s["wt_ready"], k + 1)

            def weigh(i, dst):
                return V.tensor_tensor(dst, SM[:, i, :, :, :],
                                       wt[:, :, i, :].unsqueeze(3).to_broadcast([128, A, H, DH]), ALU.mult)

            def mix_streams(k):
                for i in range(DVE_STREAMS + 1):
                    if i == 0:
                        weigh(0, acc[:, 0, :, :, :])
                        link(weigh(1, prod[:, 1, :, :, :]))
                        continue
                    if i == DVE_STREAMS:
                        eng.wait_ge(s["pool_mix"], 5 * k + 5)
                    other = prod[:, i % 2, :, :, :] if i < DVE_STREAMS else pmix[:, 0, :, :, :]
                    t = V.tensor_tensor(acc[:, i % 2, :, :, :], acc[:, (i - 1) % 2, :, :, :], other, ALU.add)
                    if i < DVE_STREAMS - 1:
                        t = weigh(i + 1, prod[:, (i + 1) % 2, :, :, :])
                    link(t)

            def mix_norm(step):
                o = acc[:, DVE_STREAMS % 2, :, :, :]
                pr = prod[:, 0, :, :, :]
                if step == 0:
                    link(V.tensor_tensor(pr, o, o, ALU.mult))
                    link(V.tensor_reduce(out=ss[:, :, :], in_=pr, op=ALU.add, axis=AX.X))
                    link(V.tensor_scalar(rs[:, 0, 0:A * H], ss[:, :, :].rearrange("p a h -> p (a h)"), 1.0 / DH, RMS_EPS, ALU.mult, ALU.add))
                else:
                    inv_sqrt(A * H)
                    V.tensor_tensor(pr, o, rs[:, 1, 0:A * H].rearrange("p (a h) -> p a h", a=A).unsqueeze(3).to_broadcast([128, A, H, DH]), ALU.mult).then_inc(s["mixed"], 1)

            def residual(k, step):
                y = lambda a: bank(6)[:, 128 * a:128 * a + 128]
                x = lambda a: x1[:, a, :]
                if step == 0:
                    eng.wait_ge(s["y_ps"], k + 1)
                    moments(y)
                elif step == 1 or step == 4:
                    inv_sqrt(A)
                elif step == 2:
                    link(scaled(y, y1))
                    link(V.tensor_tensor(x1[:, :, :], y1[:, :, :], x_all[:, bass.ds(k, 1), :, :].rearrange("p k a d -> p (k a) d"), ALU.add))
                elif step == 3:
                    moments(x)
                else:
                    scaled(x, x2n).then_inc(s["x2_ready"], 1)

            def router(k):
                eng.wait_ge(s["router_ps"], k + 1)
                link(V.tensor_copy(rl[:, :, :], bank(6)[:, 0:A * E].rearrange("p (a e) -> p a e", a=A)))
                carry_wait()
                for a in range(A):
                    t = V.max(top8[:, a, :], rl[:, a, :])
                link(t)
                V.tensor_tensor(rrep[:, :, :], rl[:, :, :], top8[:, :, 0:1].to_broadcast([128, A, E]), ALU.subtract).then_inc(s["re_in"], 1)
                V.tensor_copy(want2[:, :, 0:2], top8[:, :, 0:2])
                link(V.memset(want2[:, :, 2:8], 3.0e38))
                carry_wait()
                for a in range(A):
                    t = V.match_replace(out=cwr[:, 0, a, :], in_to_replace=want2[:, a, :], in_values=rl[:, a, :], imm_value=-3.0e38)
                link(t)
                link(V.tensor_tensor(cwr[:, 1, :, :], rl[:, :, :], cwr[:, 0, :, :], ALU.is_gt))

            def router_shares(k):
                eng.wait_ge(s["re_out"], k + 1)
                link(V.tensor_reduce(out=rsum[:, :], in_=re[:, :, :], op=ALU.add, axis=AX.X))
                link(V.reciprocal(rsum[:, :], rsum[:, :]))
                link(V.tensor_tensor(cw[:, :, :], re[:, :, :], cwr[:, 1, :, :], ALU.mult))
                link(V.tensor_tensor(cw[:, :, :], cw[:, :, :], rsum[:, :].unsqueeze(2).to_broadcast([128, A, E]), ALU.mult))
                link(V.tensor_copy(cw3[:, :, 0, :], cw[:, :, :]))
                link(V.tensor_tensor(cwr[:, 0, :, :], cw[:, :, :], cw3[:, :, 0, :], ALU.subtract))
                link(V.tensor_copy(cw3[:, :, 1, :], cwr[:, 0, :, :]))
                link(V.tensor_tensor(cwr[:, 1, :, :], cwr[:, 0, :, :], cw3[:, :, 1, :], ALU.subtract))
                V.tensor_copy(cw3[:, :, 2, :], cwr[:, 1, :, :]).then_inc(s["cw_ready"], 1)

            def router_rows(k):
                eng.wait_ge(s["cwT_ps"], k + 1)
                V.tensor_copy(cwT[:, :], bank(6)[0:48, 0:256].bitcast(bf16)).then_inc(s["cwT_ready"], 1)

            def weigh_expert(k, j):
                eng.wait_ge(s["sg_ready"], (PAIRS + 1) * k + j + 1)
                if j > 0:
                    eng.wait_ge(s["wts_ps"], PAIRS * k + j)
                    V.tensor_tensor(sc[:, j % 2, :], sg[:, j % 2, :], bank(6), ALU.mult).then_inc(s["sc_ready"], 1)

            def expert_hidden(k, j):
                n = (PAIRS + 1) * k + j
                if j > 0:
                    eng.wait_ge(s["sc_ready"], PAIRS * k + j)
                eng.wait_ge(s["up_ps"], n + 1)
                a_ = sc if j > 0 else sg
                if j >= 2:
                    carry_wait()
                    eng.wait_ge(s["z_ps"], n - 1)
                V.tensor_tensor(hT[:, j % 2, :], a_[:, j % 2, :], bank(4), ALU.mult).then_inc(s["h_ready"], 1)

            def result(k):
                eng.wait_ge(s["yo_ps"], k + 1)
                link(layer_norm(lambda a: bank(6)[:, 128 * a:128 * a + 128], y1))
                V.tensor_tensor(x_all[:, bass.ds(k, 1), :, :].rearrange("p k a d -> p (k a) d"), y1[:, :, :], x1[:, :, :], ALU.add).then_inc(s["y_ready"], 1)

            def between_levels(k, i):
                if i < 6:
                    residual(k, i)
                elif i == 8:
                    router(k)
                elif i == 9:
                    router_shares(k)
                elif i == 11:
                    weigh_expert(k, 0)
                    expert_hidden(k, 0)
                elif i == 12:
                    router_rows(k)

            def next_norm(k, n):
                if n == 2 and isinstance(k, int):
                    eng.wait_ge(x_in, 32 * (TILES - 1))
                if n in (2, 4, 6):
                    norm_x(k + 1, n // 2 - 1)

            def tile(at, one_, two):
                base[0], cnt[0] = at, 0
                if two is not None:
                    logits_out(two)
                    mix_weights(two)
                    mix_streams(two)
                if one_ is not None:
                    inverse_norms(one_)
                if two is not None:
                    mix_norm(0)
                if one_ is not None:
                    values_and_beta(one_)
                    normalise(one_)
                if two is not None:
                    mix_norm(1)
                if one_ is not None:
                    gram_out(one_)
                for i in range(LEVEL_STEPS):
                    if one_ is not None:
                        level(one_, i)
                    if two is not None:
                        between_levels(two, i)
                for n in range(NCH):
                    if one_ is not None:
                        scan_r(one_, n)
                        next_norm(one_, n)
                    if two is not None:
                        weigh_expert(two, n + 1)
                    if one_ is not None:
                        scan_s(one_, n)
                    if two is not None:
                        expert_hidden(two, n + 1)
                    if one_ is not None:
                        statistics(one_, n)
                if one_ is not None:
                    delta_out(one_)
                    delta_statistics(one_)
                if two is not None:
                    result(two)
                return cnt[0]

            eng.wait_ge(taps_in, 256)
            for m in range(POOL_TOEP, MX):
                for i in range(4):
                    if m < MS[i]:
                        for a in range(A):
                            t = toeplitz(V, m, i, a)
            t.then_inc(toep_ready, 1)
            at = cnt[0]
            at += tile(at, 0, None)
            late_weights()
            with eng.Fori(1, TILES) as k:
                assert tile(at + LOOP_STEPS * (k - 1), k, k - 1) == LOOP_STEPS, f"LOOP_STEPS is {cnt[0]}"
            tile(at + LOOP_STEPS * (TILES - 1), None, TILES - 1)

        @block.tensor
        def _(eng):
            T = nc.tensor
            eng.wait_ge(w_in, W_IN)
            eng.wait_ge(init, 9)

            def mm(o, lhsT, rhs, start=True, stop=True):
                return T.matmul(o, lhsT, rhs, start=start, stop=stop)

            for i in range(3):
                T.transpose(bank(0)[:, 128 * i:128 * i + 128], wraw[:, i, :], ident)
            T.transpose(bank(0)[:, 384:400], wg_raw[:, :], cst[0:E, 0:E]).then_inc(wprep_pe, 1)
            eng.wait_ge(wprep, 2)
            for i in range(3):
                mm(bank(1 + i), wrawT[:, i, :], diag[:, i, :, :].rearrange("p t n -> p (t n)")).then_inc(wprep_pe, 1)
            eng.wait_ge(wprep, 5)

            def carry_wait():
                T.matmul(bank(0)[:, 448:480], identb[:, :], identb[:, 0:32], start=True, stop=True)

            def mm4(o, lhsT, rhs, start=True, stop=True):
                for h in range(H):
                    q = slice(32 * h, 32 * h + 32)
                    t = T.matmul(o[q, :], lhsT[q, :], rhs[q, :], start=start, stop=stop, tile_position=(32 * h, 32 * h))
                return t

            def transposes(n, src, cols=128):
                for a in range(A):
                    t = T.transpose(bank(n)[0:cols, 128 * a:128 * a + 128], src(a), ident)
                return t

            def flat(ap):
                return ap.rearrange("p h c -> p (h c)")

            def x_transposes(k):
                eng.wait_ge(s["xn_ready"], k + 1)
                transposes(0, lambda a: xn[:, a, :]).then_inc(s["xnT_ps"], 1)

            def projection(k, n, i, taps=range(4)):
                for tap in taps:
                    t = mm(bank(n), wtap[:, i, tap, :], xnT[:, :, tap:tap + TB], start=tap == 0, stop=tap == 3)
                if tap == 3:
                    t.then_inc(s["v_ps" if i == 2 else "kq_ps"], 1)

            def projection_v(k):
                eng.wait_ge(s["xnT_ready"], k + 1)
                if not isinstance(k, int):
                    eng.wait_ge(s["vt_out"], k)
                    eng.wait_ge(s["dt_out"], k)
                projection(k, 3, 2, range(0, 1))

            def projection_vkq(k):
                projection(k, 3, 2, range(2, 4))
                projection(k, 1, 1)
                mm(bank(0), flat(wb_rep[:, :, :]), xnT[:, :, 3:3 + TB]).then_inc(s["beta_ps"], 1)
                projection(k, 2, 0)

            def square_sums(k):
                for i in range(2):
                    eng.wait_ge(s["sq_done"], 2 * k + i + 1)
                    for a in range(A):
                        c = H * (A * i + a)
                        t = mm(bank(1)[:, c:c + H], sq[:, i, 128 * a:128 * a + 128], cst[:, C_ONES:C_ONES + 128:DH])
                t.then_inc(s["ssq_ps"], 1)

            def norm_rows(k):
                eng.wait_ge(s["rn_ready"], k + 1)
                T.transpose(bank(1)[0:2 * A * H, 128:256], rs[:, 3, :], ident).then_inc(s["rnT_ps"], 1)
                eng.wait_ge(s["vP_done"], k + 1)
                eng.wait_ge(s["rnT_ready"], k + 1)
                for i in range(2):
                    for a in range(A):
                        t = mm(bank(1 + i)[:, 128 * a:128 * a + 128], headsel[:, A * i + a, :], rnT[:, :])
                t.then_inc(s["rnF_ps"], 1)

            def grams(k):
                eng.wait_ge(s["kq_ready"], k + 1)
                carry_wait()
                for g in range(G):
                    t = mm4(PS[:, 512 + 64 * g:512 + 64 * g + 64], kq[:, g, 0, :], kq[:, g, :, :].rearrange("p w i -> p (w i)"))
                t.then_inc(s["gram_ps"], 1)

            def level(k, i):
                l, f = 1 + i // 4, i % 2
                if i % 4 < 2:
                    eng.wait_ge(s["x_ready"], 10 * k + 2 * (l - 1) + f + 1)
                    lhsT, rhs, at, done = LT, X, 0, "m1_ps"
                else:
                    eng.wait_ge(s["m1_ready"], 8 * k + 2 * (l - 1) + f + 1)
                    lhsT, rhs, at, done = XT, M1, 256, "m2_ps"
                carry_wait()
                for g in range(8):
                    t = mm4(bank(1 + f)[:, at + 32 * g:at + 32 * g + 32], lhsT[:, 8 * f + g, :], rhs[:, 8 * f + g, :])
                t.then_inc(s[done], 1)

            def fir_step(k, h, m):
                if m == 0 and h == 2:
                    eng.wait_ge(s["v4_ready"], 2 * k + 2)
                if m == 0 and h == 0:
                    eng.wait_ge(s["v4_ready"], 2 * k + 1)
                    if isinstance(k, int):
                        eng.wait_ge(toep_ready, 2)
                    else:
                        eng.wait_ge(s["z_ready"], k)
                w = 128 * sum(m < x for x in MS)
                t = mm(bank(FIR_BANKS[h])[:, 0:w], v4[:, h, 8 - m:8 - m + Q, :].rearrange("p q b -> p (q b)"),
                       toep[m][:, h, :, :, :].rearrange("p s a c -> p (s a c)"), start=m == 0, stop=m == MX - 1)
                if m == MX - 1:
                    t.then_inc(s["fir_ps"], 1)

            def fir(k, h, first=0, last=MX):
                for m in range(first, last):
                    fir_step(k, h, m)

            def scan(k, n, filler):
                sn = NCH * k + n
                eng.wait_ge(s["s_ready"], sn + 1)
                gs = [(b, b * NCH + n) for b in range(NB)]
                carry_wait()
                for b, g in gs:
                    t = mm4(bank(0)[:, 32 * b:32 * b + 32], kq[:, g, 0, :], S[:, n % 2, b, :])
                t.then_inc(s["ks_ps"], 1)
                filler(0)
                eng.wait_ge(s["r_ready"], sn + 1)
                carry_wait()
                for b, g in gs:
                    t = mm4(bank(0)[:, 64 + 32 * b:96 + 32 * b], XT[:, g, :], r[:, b, :])
                t.then_inc(s["u_ps"], 1)
                filler(1)
                eng.wait_ge(s["u_ready"], sn + 1)
                carry_wait()
                for b, g in gs:
                    t = mm4(bank(0)[:, 128 + 32 * b:160 + 32 * b], kB[:, g, :], u[:, b, :])
                t.then_inc(s["ds_ps"], 1)
                for b, g in gs:
                    mm4(bank(3)[:, 32 * g:32 * g + 32], kq[:, g, 1, :], S[:, n % 2, b, :], stop=False)
                    t = mm4(bank(3)[:, 32 * g:32 * g + 32], attnT[:, g, :], u[:, b, :], start=False)
                if n == NCH - 1:
                    t.then_inc(s["o_ps"], 1)
                filler(2)

            def v_tokens(k):
                transposes(2, lambda a: vP[:, 128 * a:128 * a + 128]).then_inc(s["vt_ps"], 1)

            def delta_tokens(k):
                eng.wait_ge(s["oF_ready"], k + 1)
                transposes(3, lambda a: oF[:, 128 * a:128 * a + 128]).then_inc(s["dt_ps"], 1)

            def hidden_tokens(k):
                for i in range(2):
                    t = mm(bank(4 + i), g1x[:, 128 * i:128 * i + 128], xnT[:, :, 3:3 + TB], stop=False)
                t.then_inc(s["hidx_ps"], 1)

            def hidden_statistics(k):
                eng.wait_ge(s["stat_ready"], k + 1)
                T.matmul(bank(7)[:, 0:32], ident, ident[:, 0:32], start=True, stop=True)
                transposes(7, lambda a: stat[:, a, :, :].rearrange("p s h -> p (s h)"), cols=NS * H).then_inc(s["statT_ps"], 1)
                eng.wait_ge(s["statT_ready"], k + 1)
                for i in range(2):
                    mm(bank(4 + i), g1s[:, 128 * i:128 * i + 128], statT, start=False).then_inc(s["hid_ps"], 1)

            def logits(k):
                eng.wait_ge(s["hid_ready"], 2 * k + 2)
                for a in range(A):
                    for i in range(2):
                        t = mm(bank(7)[:, 28 * a:28 * a + 28], hid[:, i, 128 * a:128 * a + 128],
                               g2[:, i, :, :].rearrange("p s h -> p (s h)"), start=i == 0, stop=i == 1)
                t.then_inc(s["logit_ps"], 1)

            def mixed_transposes(k):
                eng.wait_ge(s["mixed"], k + 1)
                transposes(6, lambda a: flat(prod[:, 0, a, :, :])).then_inc(s["oT_ps"], 1)

            def output_projection(k):
                eng.wait_ge(s["oT_ready"], k + 1)
                for a in range(A):
                    t = mm(bank(6)[:, 128 * a:128 * a + 128], oT[:, 128 * a:128 * a + 128], wo[:, :])
                t.then_inc(s["y_ps"], 1)

            def x2_transposes(k):
                eng.wait_ge(s["x2_ready"], k + 1)
                transposes(6, lambda a: x2n[:, a, :]).then_inc(s["x2T_ps"], 1)

            def router(k):
                eng.wait_ge(s["x2T_ready"], k + 1)
                for a in range(A):
                    t = mm(bank(6)[:, E * a:E * a + E], x2T[:, 128 * a:128 * a + 128], wgT[:, :])
                t.then_inc(s["router_ps"], 1)

            def router_weights(k):
                eng.wait_ge(s["cw_ready"], k + 1)
                for a in range(A):
                    t = T.transpose(bank(6)[:, 0:256].bitcast(bf16)[:, 128 * a:128 * a + 128],
                                    cw3[:, a, :, :].rearrange("p c e -> p (c e)"), identb[:, :])
                t.then_inc(s["cwT_ps"], 1)

            def expert_gate(k, j):
                if j > 0:
                    eng.wait_ge(s["sg_ready"], (PAIRS + 1) * k + j)
                mm(bank(5), flat(w1[:, j - 1, 1, :, :]) if j else ws1[:, HS:2 * HS], x2T[:, :]).then_inc(s["gate_ps"], 1)

            def expert_weights(k, j):
                if j == 1:
                    eng.wait_ge(s["cwT_ready"], k + 1)
                else:
                    eng.wait_ge(s["sc_ready"], PAIRS * k + j - 1)
                mm(bank(6), selb[:, j - 1, :], cwT[:, :]).then_inc(s["wts_ps"], 1)

            def expert_up(k, j):
                if j > 0:
                    eng.wait_ge(s["h_ready"], (PAIRS + 1) * k + j)
                mm(bank(4), flat(w1[:, j - 1, 0, :, :]) if j else ws1[:, 0:HS], x2T[:, :]).then_inc(s["up_ps"], 1)

            def expert_down(k, j):
                eng.wait_ge(s["h_ready"], (PAIRS + 1) * k + j + 1)
                mm(bank(7), w2[:, j - 1, :] if j else ws2[:, :], hT[:, j % 2, :],
                   start=j == 0, stop=j == PAIRS).then_inc(s["z_ps"], 1)

            def expert_tokens(k):
                eng.wait_ge(s["zT_ready"], k + 1)
                transposes(6, lambda a: zT[:, 128 * a:128 * a + 128]).then_inc(s["yo_ps"], 1)

            def tile(one_, two):
                if two is not None:
                    hidden_tokens(two)
                if one_ is not None:
                    x_transposes(one_)
                if two is not None:
                    hidden_statistics(two)
                if one_ is not None:
                    projection_v(one_)
                    projection(one_, 3, 2, range(1, 2))
                if two is not None:
                    logits(two)
                if one_ is not None:
                    projection_vkq(one_)
                    square_sums(one_)
                    fir(one_, 0, 0, 4)
                    norm_rows(one_)
                    fir(one_, 0, 4)
                    grams(one_)
                    fir(one_, 1, 0, 2)
                if two is not None:
                    mixed_transposes(two)
                if one_ is not None:
                    fir(one_, 1, 2)
                if two is not None:
                    output_projection(two)
                for i in range(LEVEL_STEPS):
                    if one_ is not None:
                        level(one_, i)
                        if i < 6:
                            for m in ((0, 3), (1, 4), (2, 5, 6, 7, 8))[i % 3]:
                                fir_step(one_, 2 + i // 3, m)
                    if two is not None:
                        if i == 6:
                            x2_transposes(two)
                        elif i == 7:
                            router(two)
                        elif i == 9:
                            if one_ is not None:
                                eng.wait_ge(s["fir_out"], H * one_ + H)
                            expert_gate(two, 0)
                            expert_up(two, 0)
                        elif i == 11:
                            router_weights(two)
                if one_ is not None:
                    eng.wait_ge(s["T_ready"], 2 * one_ + 2)
                    eng.wait_ge(s["fir_out"], H * one_ + H)
                    v_tokens(one_)

                def filler(i):
                    if two is not None and i == 0:
                        expert_weights(two, n + 1)
                        expert_gate(two, n + 1)
                    elif two is not None and i == 1:
                        expert_up(two, n + 1)
                    elif two is not None:
                        expert_down(two, n)
                for n in range(NCH):
                    if one_ is not None:
                        scan(one_, n, filler)
                    else:
                        for i in range(3):
                            filler(i)
                if two is not None:
                    expert_down(two, PAIRS)
                if one_ is not None:
                    delta_tokens(one_)
                if two is not None:
                    expert_tokens(two)

            tile(0, None)
            eng.wait_ge(w_late, W_LATE)
            eng.wait_ge(wprep, 6)
            with eng.Fori(1, TILES) as k:
                tile(k, k - 1)
            tile(None, TILES - 1)


LOOP_STEPS = 116

_INS = ["hidden_states", "w_q", "w_k", "w_v", "w_b", "conv_q_w", "conv_k_w", "conv_v_w", "fir1", "fir3", "fir7",
        "fir15", "fir31", "gate_w1", "gate_b1", "gate_w2", "gate_b2", "norm_w", "w_o"]
_FFN = ["Wg", "W1", "W2", "Ws1", "Ws2"]


def kernel(**inputs):
    import numpy as _np
    import concourse.bacc as _bacc
    from concourse import mybir as _mybir
    from concourse.bass_utils import run_bass_kernel_spmd as _run

    nc = _bacc.Bacc("TRN2", target_bir_lowering=False, num_devices=1)
    arrays, args = {}, []
    for name in ["L0_attn_" + n for n in _INS] + ["L0_ffn_" + n for n in _FFN]:
        arrays[name] = _np.ascontiguousarray(inputs[name])
    arrays["shape_constants"] = shape_constants()
    for name, a in arrays.items():
        args.append(nc.dram_tensor(name, a.shape, _mybir.dt.from_np(a.dtype), kind="ExternalInput").ap())
    out = nc.dram_tensor("out", (NB, SEQ, D), _mybir.dt.float32, kind="ExternalOutput").ap()
    build(nc, *args, out)
    r = _run(nc, [arrays], core_ids=[0])
    return r.results[0]["out"]
```
